# Optimizing a Trainium2 kernel written in Bass

```python
import numpy as np
import jax
import jax.numpy as jnp

def _softmax(x, axis=-1):
    return jax.nn.softmax(x, axis=axis)

def _gelu(x):
    return jax.nn.gelu(x, approximate=True)

def _silu(x):
    return jax.nn.silu(x)

def _sigmoid(x):
    return jax.nn.sigmoid(x)

def _layernorm(x, axis=-1, eps=1e-05):
    m = jnp.mean(x, axis=axis, keepdims=True)
    v = jnp.var(x, axis=axis, keepdims=True)
    return (x - m) / jnp.sqrt(v + eps)

def _scatter_add(tgt, idx, src, axis=0):
    return tgt.at[idx].add(src)

def _segment_sum(src, seg, n):
    return jax.ops.segment_sum(src, seg, n)
kernel_name = 'mk_recurrent_d4_jaxref_r8_b3cdcc'

def setup_inputs(seed: int=0):
    np.random.seed(seed)
    _w = jnp.asarray

    def _L0_attn_setup():
        import jax, jax.numpy as jnp
        import numpy as np
        D_MODEL = 128
        N_HEADS = 16
        D_K = D_MODEL // N_HEADS
        WINDOW = 64
        ROPE_BASE = 10000.0

        def _apply_rope(x):
            S, D = (x.shape[2], x.shape[3])
            half = D // 2
            inv_freq = 1.0 / ROPE_BASE ** (jnp.arange(half, dtype=jnp.float32) / half)
            ang = jnp.arange(S, dtype=jnp.float32)[:, None] * inv_freq[None, :]
            cos = jnp.cos(ang).astype(x.dtype)
            sin = jnp.sin(ang).astype(x.dtype)
            x_even = x[..., ::2]
            x_odd = x[..., 1::2]
            out_even = x_even * cos - x_odd * sin
            out_odd = x_odd * cos + x_even * sin
            return jnp.stack([out_even, out_odd], axis=-1).reshape(x.shape)
        key = jax.random.key(seed)
        k1, k2, k3 = jax.random.split(key, 3)
        B, S = (2, 256)
        x = jax.random.normal(k1, (B, S, D_MODEL), dtype=jnp.float32)
        w_qkv = jax.random.normal(k2, (D_MODEL, 3 * D_MODEL), dtype=jnp.float32) * D_MODEL ** (-0.5)
        w_o = jax.random.normal(k3, (D_MODEL, D_MODEL), dtype=jnp.float32) * D_MODEL ** (-0.5)
        return {'x': x, 'w_qkv': w_qkv, 'w_o': w_o}
    _L0_attn_in = _L0_attn_setup()

    def _L0_ffn_setup():
        import jax, jax.numpy as jnp
        import numpy as np
        DIM = 128
        DEPTH = 2
        HEADS = 8
        DIM_HEAD = 64
        WINDOW = 64
        INNER = HEADS * DIM_HEAD
        HID = int(DIM * 4 * 2 / 3)
        B, N = (2, 1024)
        QK_SCALE = 8.0

        def shift_token(t):
            t1, t2 = jnp.split(t, 2, axis=-1)
            t2 = jnp.pad(t2, ((0, 0), (1, 0), (0, 0)))[:, :-1]
            return jnp.concatenate([t1, t2], axis=-1)

        def l2norm(t):
            return t / jnp.clip(jnp.linalg.norm(t, axis=-1, keepdims=True), 1e-12)

        def rotate_half(x):
            x1, x2 = jnp.split(x, 2, axis=-1)
            return jnp.concatenate([-x2, x1], axis=-1)

        def rotary_xpos(q, k):
            n = q.shape[-2]
            half_idx = jnp.arange(0, DIM_HEAD, 2, dtype=jnp.float32)
            inv_freq = 1.0 / 10000.0 ** (half_idx / DIM_HEAD)
            t = jnp.arange(n, dtype=jnp.float32)
            freqs = t[:, None] * inv_freq[None, :]
            freqs = jnp.concatenate([freqs, freqs], axis=-1)
            base = (half_idx + 0.4 * DIM_HEAD) / (1.4 * DIM_HEAD)
            power = (t - n // 2) / float(WINDOW // 2)
            scale = base[None, :] ** power[:, None]
            scale = jnp.concatenate([scale, scale], axis=-1)
            cos, sin = (jnp.cos(freqs), jnp.sin(freqs))
            q = q * cos * scale + rotate_half(q) * sin * scale
            k = k * cos / scale + rotate_half(k) * sin / scale
            return (q, k)

        def local_attention(q, k, v):
            b, h, n, d = q.shape
            w = n // WINDOW
            bq = q.reshape(b, h, w, WINDOW, d) * QK_SCALE
            bk = k.reshape(b, h, w, WINDOW, d)
            bv = v.reshape(b, h, w, WINDOW, d)

            def look_around(t):
                p = jnp.pad(t, ((0, 0), (0, 0), (1, 0), (0, 0), (0, 0)))
                return jnp.concatenate([p[:, :, :w], p[:, :, 1:]], axis=3)
            bk, bv = (look_around(bk), look_around(bv))
            bt = jnp.arange(n).reshape(w, WINDOW)
            btp = jnp.pad(bt, ((1, 0), (0, 0)), constant_values=-1)
            btk = jnp.concatenate([btp[:w], btp[1:]], axis=1)
            sim = jnp.einsum('bhwid,bhwjd->bhwij', bq, bk)
            i = bt[:, :, None]
            j = btk[:, None, :]
            mask = (i < j) | (i > j + WINDOW) | (j == -1)
            sim = jnp.where(mask, -jnp.finfo(sim.dtype).max, sim)
            attn = jax.nn.softmax(sim, axis=-1)
            out = jnp.einsum('bhwij,bhwjd->bhwid', attn, bv)
            return out.reshape(b, h, n, d)

        def _layer(x, wqkv, qs, ksc, wo, lg, lb, w1, b1, w2, b2):
            b, n, _ = x.shape
            h = shift_token(x)
            qkv = h @ wqkv
            q, k, v = jnp.split(qkv, 3, axis=-1)
            to_heads = lambda t: t.reshape(b, n, HEADS, DIM_HEAD).transpose(0, 2, 1, 3)
            q, k, v = (to_heads(q), to_heads(k), to_heads(v))
            q = l2norm(q) * qs
            k = l2norm(k) * ksc
            q, k = rotary_xpos(q, k)
            o = local_attention(q, k, v)
            o = o.transpose(0, 2, 1, 3).reshape(b, n, INNER)
            x = x + o @ wo
            h = shift_token(x)
            mu = h.mean(-1, keepdims=True)
            var = h.var(-1, keepdims=True)
            h = (h - mu) / jnp.sqrt(var + 1e-05) * lg + lb
            h = h @ w1 + b1
            a, g = jnp.split(h, 2, axis=-1)
            h = a * jax.nn.gelu(g, approximate=False)
            x = x + h @ w2 + b2
            return x
        key = jax.random.key(seed)
        ks = jax.random.split(key, 6)
        return {'x': jax.random.normal(ks[0], (B, N, DIM), jnp.float32), 'wqkv': jax.random.normal(ks[1], (DEPTH, DIM, 3 * INNER), jnp.float32) * 0.02, 'q_scale': jnp.ones((DEPTH, DIM_HEAD), jnp.float32), 'k_scale': jnp.ones((DEPTH, DIM_HEAD), jnp.float32), 'wo': jax.random.normal(ks[2], (DEPTH, INNER, DIM), jnp.float32) * 0.02, 'ln_g': jnp.ones((DEPTH, DIM), jnp.float32), 'ln_b': jnp.zeros((DEPTH, DIM), jnp.float32), 'w1': jax.random.normal(ks[3], (DEPTH, DIM, 2 * HID), jnp.float32) * 0.02, 'b1': jnp.zeros((DEPTH, 2 * HID), jnp.float32), 'w2': jax.random.normal(ks[4], (DEPTH, HID, DIM), jnp.float32) * 0.02, 'b2': jnp.zeros((DEPTH, DIM), jnp.float32)}
    _L0_ffn_in = _L0_ffn_setup()

    def _L1_attn_setup():
        import jax, jax.numpy as jnp
        import numpy as np
        import math
        B, S, E = (2, 256, 128)
        H, DC, DR = (16, 32, 128)
        HD = E // H

        def _linear_params(key, din, dout):
            k1, k2 = jax.random.split(key)
            bound = 1.0 / math.sqrt(din)
            w = jax.random.uniform(k1, (din, dout), minval=-bound, maxval=bound, dtype=jnp.float32)
            b = jax.random.uniform(k2, (dout,), minval=-bound, maxval=bound, dtype=jnp.float32)
            return (w, b)

        def _gelu(x):
            return jax.nn.gelu(x, approximate=False)

        def _rope_cos_sin(seq_len, d_rope):
            inv_freq = 1.0 / 10000.0 ** (jnp.arange(0, d_rope, 2, dtype=jnp.float32) / d_rope)
            t = jnp.arange(seq_len, dtype=jnp.float32)
            freqs = t[:, None] * inv_freq[None, :]
            emb = jnp.concatenate([freqs, freqs], axis=-1)
            return (jnp.cos(emb), jnp.sin(emb))

        def _apply_rope(x, cos, sin):
            d = x.shape[-1]
            x1, x2 = (x[..., :d // 2], x[..., d // 2:])
            rot = jnp.concatenate([-x2, x1], axis=-1)
            return x * cos + rot * sin
        key = jax.random.key(seed)
        ks = jax.random.split(key, 10)
        x = jax.random.normal(ks[0], (B, S, E), dtype=jnp.float32)
        wq, bq = _linear_params(ks[1], E, DC)
        wqc, bqc = _linear_params(ks[2], DC, E - DR)
        wqr, bqr = _linear_params(ks[3], E, DR)
        wkv, bkv = _linear_params(ks[4], E, DC)
        wkr, bkr = _linear_params(ks[5], E, DR)
        wkc, bkc = _linear_params(ks[6], DC, E - DR)
        wv, bv = _linear_params(ks[7], DC, E)
        wo, bo = _linear_params(ks[8], E, E)
        return dict(x=x, wq=wq, bq=bq, wqc=wqc, bqc=bqc, wqr=wqr, bqr=bqr, wkv=wkv, bkv=bkv, wkr=wkr, bkr=bkr, wkc=wkc, bkc=bkc, wv=wv, bv=bv, wo=wo, bo=bo)
    _L1_attn_in = _L1_attn_setup()

    def _L1_ffn_setup():
        import jax, jax.numpy as jnp
        import numpy as np
        H = 8
        KD = 128
        TOPK = 8
        NUM_KEYS = 32
        N_EXPERTS = NUM_KEYS * NUM_KEYS
        N_DIM = 128
        BN_EPS = 1e-05

        def gelu_new(x):
            c = jnp.sqrt(jnp.asarray(2.0 / jnp.pi, x.dtype))
            return 0.5 * x * (1.0 + jnp.tanh(c * (x + 0.044715 * x * x * x)))
        key = jax.random.key(seed)
        ks = jax.random.split(key, 5)
        b, s = (2, 128)
        x = jax.random.normal(ks[0], (b, s, N_DIM), dtype=jnp.float32)
        w_q = jax.random.normal(ks[1], (N_DIM, 2 * H * KD), dtype=jnp.float32) * 0.02
        bn_gamma = jnp.ones((2 * H * KD,), dtype=jnp.float32)
        bn_beta = jnp.zeros((2 * H * KD,), dtype=jnp.float32)
        keys = jax.random.normal(ks[2], (H, NUM_KEYS, 2, KD), dtype=jnp.float32) * 0.02
        down_embed = jax.random.normal(ks[3], (N_EXPERTS, N_DIM), dtype=jnp.float32) * 0.02
        up_embed = jax.random.normal(ks[4], (N_EXPERTS, N_DIM), dtype=jnp.float32) * 0.02
        return {'x': x, 'w_q': w_q, 'bn_gamma': bn_gamma, 'bn_beta': bn_beta, 'keys': keys, 'down_embed': down_embed, 'up_embed': up_embed}
    _L1_ffn_in = _L1_ffn_setup()

    def _L2_attn_setup():
        import jax, jax.numpy as jnp
        import numpy as np
        T, B, H = (128, 32, 128)
        key = jax.random.key(seed)
        k1, k2, k3, k4 = jax.random.split(key, 4)
        s = 1.0 / np.sqrt(H)
        return {'inputs': jax.random.normal(k1, (T, B, H), dtype=jnp.float32), 'W': jax.random.normal(k2, (H, H), dtype=jnp.float32) * s, 'proj': jax.random.normal(k3, (H,), dtype=jnp.float32) * s, 'concat_w': jax.random.normal(k4, (H, 2 * H), dtype=jnp.float32) * s, 'concat_b': jnp.zeros((H,), dtype=jnp.float32)}
    _L2_attn_in = _L2_attn_setup()

    def _L2_ffn_setup():
        import jax, jax.numpy as jnp
        import numpy as np
        key = jax.random.key(seed)
        kx, kw = jax.random.split(key)
        x = jax.random.normal(kx, (32, 512, 128), dtype=jnp.float32)
        weight = jax.random.normal(kw, (128, 128), dtype=jnp.float32) * 0.01
        return {'x': x, 'weight': weight}
    _L2_ffn_in = _L2_ffn_setup()

    def _L3_attn_setup():
        import jax, jax.numpy as jnp
        import numpy as np
        DIM = 128
        H = 16
        HD = DIM // H // 2
        LAMBDA_INIT = 0.8 - 0.6 * float(np.exp(-0.3 * 0))
        EPS = 1e-05

        def _rms_norm(x, w, eps):
            return x * jax.lax.rsqrt(jnp.mean(jnp.square(x), axis=-1, keepdims=True) + eps) * w
        key = jax.random.key(seed)
        ks = jax.random.split(key, 9)
        B, N = (4, 512)
        return {'x': jax.random.normal(ks[0], (B, N, DIM), jnp.float32), 'w_qkv': jax.random.normal(ks[1], (3 * DIM, DIM), jnp.float32) * 0.02, 'w_proj': jax.random.normal(ks[2], (DIM, DIM), jnp.float32) * 0.02, 'b_proj': jnp.zeros((DIM,), jnp.float32), 'lambda_q1': jax.random.normal(ks[3], (HD,), jnp.float32) * 0.1, 'lambda_k1': jax.random.normal(ks[4], (HD,), jnp.float32) * 0.1, 'lambda_q2': jax.random.normal(ks[5], (HD,), jnp.float32) * 0.1, 'lambda_k2': jax.random.normal(ks[6], (HD,), jnp.float32) * 0.1, 'sub_norm_w': jnp.ones((2 * HD,), jnp.float32)}
    _L3_attn_in = _L3_attn_setup()

    def _L3_ffn_setup():
        import jax, jax.numpy as jnp
        import numpy as np
        B, S, H, M, E, K = (4, 256, 128, 512, 8, 2)
        key = jax.random.key(seed)
        ks = jax.random.split(key, 6)
        x = jax.random.normal(ks[0], (B, S, H), dtype=jnp.float32)
        Wr = jax.random.normal(ks[1], (E, H), dtype=jnp.float32) * (1.0 / np.sqrt(H))
        W1 = jax.random.normal(ks[2], (E, M, H), dtype=jnp.float32) * np.sqrt(2.0 / (H + M))
        b1 = jax.random.normal(ks[3], (E, M), dtype=jnp.float32) * 1e-06
        W2 = jax.random.normal(ks[4], (E, H, M), dtype=jnp.float32) * np.sqrt(2.0 / (H + M))
        b2 = jax.random.normal(ks[5], (E, H), dtype=jnp.float32) * 1e-06
        return {'x': x, 'Wr': Wr, 'W1': W1, 'b1': b1, 'W2': W2, 'b2': b2}
    _L3_ffn_in = _L3_ffn_setup()
    _d = {'L0_attn_x': _L0_attn_in['x'], 'L0_attn_w_qkv': _L0_attn_in['w_qkv'], 'L0_attn_w_o': _L0_attn_in['w_o'], 'L0_ffn_wqkv': _L0_ffn_in['wqkv'], 'L0_ffn_q_scale': _L0_ffn_in['q_scale'], 'L0_ffn_k_scale': _L0_ffn_in['k_scale'], 'L0_ffn_wo': _L0_ffn_in['wo'], 'L0_ffn_ln_g': _L0_ffn_in['ln_g'], 'L0_ffn_ln_b': _L0_ffn_in['ln_b'], 'L0_ffn_w1': _L0_ffn_in['w1'], 'L0_ffn_b1': _L0_ffn_in['b1'], 'L0_ffn_w2': _L0_ffn_in['w2'], 'L0_ffn_b2': _L0_ffn_in['b2'], 'L1_attn_wq': _L1_attn_in['wq'], 'L1_attn_bq': _L1_attn_in['bq'], 'L1_attn_wqc': _L1_attn_in['wqc'], 'L1_attn_bqc': _L1_attn_in['bqc'], 'L1_attn_wqr': _L1_attn_in['wqr'], 'L1_attn_bqr': _L1_attn_in['bqr'], 'L1_attn_wkv': _L1_attn_in['wkv'], 'L1_attn_bkv': _L1_attn_in['bkv'], 'L1_attn_wkr': _L1_attn_in['wkr'], 'L1_attn_bkr': _L1_attn_in['bkr'], 'L1_attn_wkc': _L1_attn_in['wkc'], 'L1_attn_bkc': _L1_attn_in['bkc'], 'L1_attn_wv': _L1_attn_in['wv'], 'L1_attn_bv': _L1_attn_in['bv'], 'L1_attn_wo': _L1_attn_in['wo'], 'L1_attn_bo': _L1_attn_in['bo'], 'L1_ffn_w_q': _L1_ffn_in['w_q'], 'L1_ffn_bn_gamma': _L1_ffn_in['bn_gamma'], 'L1_ffn_bn_beta': _L1_ffn_in['bn_beta'], 'L1_ffn_keys': _L1_ffn_in['keys'], 'L1_ffn_down_embed': _L1_ffn_in['down_embed'], 'L1_ffn_up_embed': _L1_ffn_in['up_embed'], 'L2_attn_W': _L2_attn_in['W'], 'L2_attn_proj': _L2_attn_in['proj'], 'L2_attn_concat_w': _L2_attn_in['concat_w'], 'L2_attn_concat_b': _L2_attn_in['concat_b'], 'L2_ffn_weight': _L2_ffn_in['weight'], 'L3_attn_w_qkv': _L3_attn_in['w_qkv'], 'L3_attn_w_proj': _L3_attn_in['w_proj'], 'L3_attn_b_proj': _L3_attn_in['b_proj'], 'L3_attn_lambda_q1': _L3_attn_in['lambda_q1'], 'L3_attn_lambda_k1': _L3_attn_in['lambda_k1'], 'L3_attn_lambda_q2': _L3_attn_in['lambda_q2'], 'L3_attn_lambda_k2': _L3_attn_in['lambda_k2'], 'L3_attn_sub_norm_w': _L3_attn_in['sub_norm_w'], 'L3_ffn_Wr': _L3_ffn_in['Wr'], 'L3_ffn_W1': _L3_ffn_in['W1'], 'L3_ffn_b1': _L3_ffn_in['b1'], 'L3_ffn_W2': _L3_ffn_in['W2'], 'L3_ffn_b2': _L3_ffn_in['b2']}
    _x0 = _d['L0_attn_x']
    _d['L0_attn_x'] = jax.random.normal(jax.random.fold_in(jax.random.key(seed), 1), (2, 1024, 128), dtype=_x0.dtype)
    del _x0
    return _d

def reference(L0_attn_x, L0_attn_w_qkv, L0_attn_w_o, L0_ffn_wqkv, L0_ffn_q_scale, L0_ffn_k_scale, L0_ffn_wo, L0_ffn_ln_g, L0_ffn_ln_b, L0_ffn_w1, L0_ffn_b1, L0_ffn_w2, L0_ffn_b2, L1_attn_wq, L1_attn_bq, L1_attn_wqc, L1_attn_bqc, L1_attn_wqr, L1_attn_bqr, L1_attn_wkv, L1_attn_bkv, L1_attn_wkr, L1_attn_bkr, L1_attn_wkc, L1_attn_bkc, L1_attn_wv, L1_attn_bv, L1_attn_wo, L1_attn_bo, L1_ffn_w_q, L1_ffn_bn_gamma, L1_ffn_bn_beta, L1_ffn_keys, L1_ffn_down_embed, L1_ffn_up_embed, L2_attn_W, L2_attn_proj, L2_attn_concat_w, L2_attn_concat_b, L2_ffn_weight, L3_attn_w_qkv, L3_attn_w_proj, L3_attn_b_proj, L3_attn_lambda_q1, L3_attn_lambda_k1, L3_attn_lambda_q2, L3_attn_lambda_k2, L3_attn_sub_norm_w, L3_ffn_Wr, L3_ffn_W1, L3_ffn_b1, L3_ffn_W2, L3_ffn_b2):

    def _L0_attn_ref(x, w_qkv, w_o):
        import jax, jax.numpy as jnp
        import numpy as np
        D_MODEL = 128
        N_HEADS = 16
        D_K = D_MODEL // N_HEADS
        WINDOW = 64
        ROPE_BASE = 10000.0

        def _apply_rope(x):
            S, D = (x.shape[2], x.shape[3])
            half = D // 2
            inv_freq = 1.0 / ROPE_BASE ** (jnp.arange(half, dtype=jnp.float32) / half)
            ang = jnp.arange(S, dtype=jnp.float32)[:, None] * inv_freq[None, :]
            cos = jnp.cos(ang).astype(x.dtype)
            sin = jnp.sin(ang).astype(x.dtype)
            x_even = x[..., ::2]
            x_odd = x[..., 1::2]
            out_even = x_even * cos - x_odd * sin
            out_odd = x_odd * cos + x_even * sin
            return jnp.stack([out_even, out_odd], axis=-1).reshape(x.shape)
        B, S, _ = x.shape
        qkv = (x @ w_qkv).reshape(B, S, 3, N_HEADS, D_K)
        qkv = jnp.transpose(qkv, (2, 0, 3, 1, 4))
        q, k, v = (qkv[0], qkv[1], qkv[2])
        q = _apply_rope(q)
        k = _apply_rope(k)
        i = jnp.arange(S)[:, None]
        j = jnp.arange(S)[None, :]
        allowed = (j <= i) & (j >= i - WINDOW)
        bias = jnp.where(allowed, 0.0, -jnp.inf).astype(x.dtype)
        scores = jnp.einsum('bhqd,bhkd->bhqk', q, k) * D_K ** (-0.5) + bias
        attn = jax.nn.softmax(scores, axis=-1)
        out = jnp.einsum('bhqk,bhkd->bhqd', attn, v)
        out = jnp.transpose(out, (0, 2, 1, 3)).reshape(B, S, D_MODEL)
        return out @ w_o

    def _L0_ffn_ref(x, wqkv, q_scale, k_scale, wo, ln_g, ln_b, w1, b1, w2, b2):
        import jax, jax.numpy as jnp
        import numpy as np
        DIM = 128
        DEPTH = 2
        HEADS = 8
        DIM_HEAD = 64
        WINDOW = 64
        INNER = HEADS * DIM_HEAD
        HID = int(DIM * 4 * 2 / 3)
        B, N = (2, 1024)
        QK_SCALE = 8.0

        def shift_token(t):
            t1, t2 = jnp.split(t, 2, axis=-1)
            t2 = jnp.pad(t2, ((0, 0), (1, 0), (0, 0)))[:, :-1]
            return jnp.concatenate([t1, t2], axis=-1)

        def l2norm(t):
            return t / jnp.clip(jnp.linalg.norm(t, axis=-1, keepdims=True), 1e-12)

        def rotate_half(x):
            x1, x2 = jnp.split(x, 2, axis=-1)
            return jnp.concatenate([-x2, x1], axis=-1)

        def rotary_xpos(q, k):
            n = q.shape[-2]
            half_idx = jnp.arange(0, DIM_HEAD, 2, dtype=jnp.float32)
            inv_freq = 1.0 / 10000.0 ** (half_idx / DIM_HEAD)
            t = jnp.arange(n, dtype=jnp.float32)
            freqs = t[:, None] * inv_freq[None, :]
            freqs = jnp.concatenate([freqs, freqs], axis=-1)
            base = (half_idx + 0.4 * DIM_HEAD) / (1.4 * DIM_HEAD)
            power = (t - n // 2) / float(WINDOW // 2)
            scale = base[None, :] ** power[:, None]
            scale = jnp.concatenate([scale, scale], axis=-1)
            cos, sin = (jnp.cos(freqs), jnp.sin(freqs))
            q = q * cos * scale + rotate_half(q) * sin * scale
            k = k * cos / scale + rotate_half(k) * sin / scale
            return (q, k)

        def local_attention(q, k, v):
            b, h, n, d = q.shape
            w = n // WINDOW
            bq = q.reshape(b, h, w, WINDOW, d) * QK_SCALE
            bk = k.reshape(b, h, w, WINDOW, d)
            bv = v.reshape(b, h, w, WINDOW, d)

            def look_around(t):
                p = jnp.pad(t, ((0, 0), (0, 0), (1, 0), (0, 0), (0, 0)))
                return jnp.concatenate([p[:, :, :w], p[:, :, 1:]], axis=3)
            bk, bv = (look_around(bk), look_around(bv))
            bt = jnp.arange(n).reshape(w, WINDOW)
            btp = jnp.pad(bt, ((1, 0), (0, 0)), constant_values=-1)
            btk = jnp.concatenate([btp[:w], btp[1:]], axis=1)
            sim = jnp.einsum('bhwid,bhwjd->bhwij', bq, bk)
            i = bt[:, :, None]
            j = btk[:, None, :]
            mask = (i < j) | (i > j + WINDOW) | (j == -1)
            sim = jnp.where(mask, -jnp.finfo(sim.dtype).max, sim)
            attn = jax.nn.softmax(sim, axis=-1)
            out = jnp.einsum('bhwij,bhwjd->bhwid', attn, bv)
            return out.reshape(b, h, n, d)

        def _layer(x, wqkv, qs, ksc, wo, lg, lb, w1, b1, w2, b2):
            b, n, _ = x.shape
            h = shift_token(x)
            qkv = h @ wqkv
            q, k, v = jnp.split(qkv, 3, axis=-1)
            to_heads = lambda t: t.reshape(b, n, HEADS, DIM_HEAD).transpose(0, 2, 1, 3)
            q, k, v = (to_heads(q), to_heads(k), to_heads(v))
            q = l2norm(q) * qs
            k = l2norm(k) * ksc
            q, k = rotary_xpos(q, k)
            o = local_attention(q, k, v)
            o = o.transpose(0, 2, 1, 3).reshape(b, n, INNER)
            x = x + o @ wo
            h = shift_token(x)
            mu = h.mean(-1, keepdims=True)
            var = h.var(-1, keepdims=True)
            h = (h - mu) / jnp.sqrt(var + 1e-05) * lg + lb
            h = h @ w1 + b1
            a, g = jnp.split(h, 2, axis=-1)
            h = a * jax.nn.gelu(g, approximate=False)
            x = x + h @ w2 + b2
            return x
        for l in range(DEPTH):
            x = _layer(x, wqkv[l], q_scale[l], k_scale[l], wo[l], ln_g[l], ln_b[l], w1[l], b1[l], w2[l], b2[l])
        return x

    def _L1_attn_ref(x, wq, bq, wqc, bqc, wqr, bqr, wkv, bkv, wkr, bkr, wkc, bkc, wv, bv, wo, bo):
        import jax, jax.numpy as jnp
        import numpy as np
        import math
        B, S, E = (2, 256, 128)
        H, DC, DR = (16, 32, 128)
        HD = E // H

        def _linear_params(key, din, dout):
            k1, k2 = jax.random.split(key)
            bound = 1.0 / math.sqrt(din)
            w = jax.random.uniform(k1, (din, dout), minval=-bound, maxval=bound, dtype=jnp.float32)
            b = jax.random.uniform(k2, (dout,), minval=-bound, maxval=bound, dtype=jnp.float32)
            return (w, b)

        def _gelu(x):
            return jax.nn.gelu(x, approximate=False)

        def _rope_cos_sin(seq_len, d_rope):
            inv_freq = 1.0 / 10000.0 ** (jnp.arange(0, d_rope, 2, dtype=jnp.float32) / d_rope)
            t = jnp.arange(seq_len, dtype=jnp.float32)
            freqs = t[:, None] * inv_freq[None, :]
            emb = jnp.concatenate([freqs, freqs], axis=-1)
            return (jnp.cos(emb), jnp.sin(emb))

        def _apply_rope(x, cos, sin):
            d = x.shape[-1]
            x1, x2 = (x[..., :d // 2], x[..., d // 2:])
            rot = jnp.concatenate([-x2, x1], axis=-1)
            return x * cos + rot * sin
        b, s, _ = x.shape
        cq = _gelu(x @ wq + bq)
        q_c = cq @ wqc + bqc
        q_r = x @ wqr + bqr
        ckv = _gelu(x @ wkv + bkv)
        k_r = x @ wkr + bkr
        k_c = ckv @ wkc + bkc
        v = (ckv @ wv + bv).reshape(b, s, H, HD).transpose(0, 2, 1, 3)
        cos, sin = _rope_cos_sin(s, DR)
        q_r = _apply_rope(q_r, cos, sin)
        k_r = _apply_rope(k_r, cos, sin)
        q = _gelu(jnp.concatenate([q_c, q_r], axis=-1)).reshape(b, s, H, HD).transpose(0, 2, 1, 3)
        k = _gelu(jnp.concatenate([k_c, k_r], axis=-1)).reshape(b, s, H, HD).transpose(0, 2, 1, 3)
        scale = 1.0 / math.sqrt(HD)
        scores = jnp.einsum('bhqd,bhkd->bhqk', q, k) * scale
        causal = jnp.triu(jnp.ones((s, s), dtype=bool), k=1)
        scores = jnp.where(causal[None, None], -jnp.inf, scores)
        attn = jax.nn.softmax(scores, axis=-1)
        out = jnp.einsum('bhqk,bhkd->bhqd', attn, v)
        out = out.transpose(0, 2, 1, 3).reshape(b, s, E)
        return out @ wo + bo

    def _L1_ffn_ref(x, w_q, bn_gamma, bn_beta, keys, down_embed, up_embed):
        import jax, jax.numpy as jnp
        import numpy as np
        H = 8
        KD = 128
        TOPK = 8
        NUM_KEYS = 32
        N_EXPERTS = NUM_KEYS * NUM_KEYS
        N_DIM = 128
        BN_EPS = 1e-05

        def gelu_new(x):
            c = jnp.sqrt(jnp.asarray(2.0 / jnp.pi, x.dtype))
            return 0.5 * x * (1.0 + jnp.tanh(c * (x + 0.044715 * x * x * x)))
        b, n, d = x.shape
        q = jnp.einsum('bnd,de->bne', x, w_q)
        mean = jnp.mean(q, axis=(0, 1))
        var = jnp.var(q, axis=(0, 1))
        q = (q - mean) * jax.lax.rsqrt(var + BN_EPS) * bn_gamma + bn_beta
        q = q.reshape(b, n, 2, H, KD).transpose(2, 0, 1, 3, 4)
        sim = jnp.einsum('pbnhd,hkpd->pbnhk', q, keys)
        sx, ix = jax.lax.top_k(sim[0], TOPK)
        sy, iy = jax.lax.top_k(sim[1], TOPK)
        all_scores = (sx[..., :, None] + sy[..., None, :]).reshape(b, n, H, TOPK * TOPK)
        all_indices = (ix[..., :, None] * NUM_KEYS + iy[..., None, :]).reshape(b, n, H, TOPK * TOPK)
        scores, pk = jax.lax.top_k(all_scores, TOPK)
        indices = jnp.take_along_axis(all_indices, pk, axis=-1)
        wd = down_embed[indices]
        wu = up_embed[indices]
        h = jnp.einsum('bnd,bnhkd->bnhk', x, wd)
        h = gelu_new(h)
        h = jax.nn.softmax(scores, axis=-1) * h
        out = jnp.einsum('bnhk,bnhkd->bnd', h, wu)
        return out

    def _L2_attn_ref(inputs, W, proj, concat_w, concat_b):
        import jax, jax.numpy as jnp
        import numpy as np
        T, B, H = (128, 32, 128)
        T_, B_, H_ = inputs.shape
        hp = jnp.tanh(jnp.einsum('sbh,hk->sbk', inputs, W))
        scores = jnp.einsum('sbk,k->sb', hp, proj)
        t_idx = jnp.arange(T_)
        mask = t_idx[None, :] < t_idx[:, None]
        neg = jnp.finfo(scores.dtype).min
        logits = jnp.where(mask[:, :, None], scores[None, :, :], neg)
        attn = jax.nn.softmax(logits, axis=1)
        context = jnp.einsum('tsb,sbh->tbh', attn, inputs)
        cat = jnp.concatenate([inputs, context], axis=-1)
        out = jnp.tanh(jnp.einsum('tbc,hc->tbh', cat, concat_w) + concat_b)
        out = out.at[:2].set(inputs[:2])
        return out

    def _L2_ffn_ref(x, weight):
        import jax, jax.numpy as jnp
        import numpy as np
        b_weight = jnp.sign(weight)
        return jnp.einsum('bsi,oi->bso', x, b_weight)

    def _L3_attn_ref(x, w_qkv, w_proj, b_proj, lambda_q1, lambda_k1, lambda_q2, lambda_k2, sub_norm_w):
        import jax, jax.numpy as jnp
        import numpy as np
        DIM = 128
        H = 16
        HD = DIM // H // 2
        LAMBDA_INIT = 0.8 - 0.6 * float(np.exp(-0.3 * 0))
        EPS = 1e-05

        def _rms_norm(x, w, eps):
            return x * jax.lax.rsqrt(jnp.mean(jnp.square(x), axis=-1, keepdims=True) + eps) * w
        B, N, C = x.shape
        scale = HD ** (-0.5)
        qkv = x @ w_qkv.T
        q, k, v = jnp.split(qkv, 3, axis=-1)
        q = q.reshape(B, N, H, 2, HD)
        k = k.reshape(B, N, H, 2, HD)
        v = v.reshape(B, N, H, 2 * HD)
        lam = jnp.exp(jnp.sum(lambda_q1 * lambda_k1)) - jnp.exp(jnp.sum(lambda_q2 * lambda_k2)) + LAMBDA_INIT

        def sdpa(qi, ki):
            s = jnp.einsum('bnhd,bmhd->bhnm', qi, ki) * scale
            p = jax.nn.softmax(s, axis=-1)
            return jnp.einsum('bhnm,bmhe->bhne', p, v)
        a1 = sdpa(q[:, :, :, 0], k[:, :, :, 0])
        a2 = sdpa(q[:, :, :, 1], k[:, :, :, 1])
        o = a1 - lam * a2
        o = _rms_norm(o, sub_norm_w, EPS) * (1.0 - LAMBDA_INIT)
        o = o.transpose(0, 2, 1, 3).reshape(B, N, C)
        return o @ w_proj.T + b_proj

    def _L3_ffn_ref(x, Wr, W1, b1, W2, b2):
        import jax, jax.numpy as jnp
        import numpy as np
        B, S, H, M, E, K = (4, 256, 128, 512, 8, 2)
        logits = jnp.einsum('bsh,eh->bse', x, Wr)
        probs = jax.nn.softmax(logits, axis=-1)
        top_v, top_i = jax.lax.top_k(probs, K)
        top_v = top_v / jnp.sum(top_v, axis=-1, keepdims=True)
        out = jnp.zeros_like(x)
        for e in range(E):
            w_e = jnp.sum(jnp.where(top_i == e, top_v, 0.0), axis=-1)
            h = jnp.einsum('bsh,mh->bsm', x, W1[e]) + b1[e]
            h = jax.nn.gelu(h, approximate=False)
            y = jnp.einsum('bsm,hm->bsh', h, W2[e]) + b2[e]
            out = out + y * w_e[..., None]
        return out
    x = L0_attn_x
    xn = _layernorm(x, axis=-1)
    s = _L0_attn_ref(xn, L0_attn_w_qkv, L0_attn_w_o)
    g = _silu(_L0_ffn_ref(xn, L0_ffn_wqkv, L0_ffn_q_scale, L0_ffn_k_scale, L0_ffn_wo, L0_ffn_ln_g, L0_ffn_ln_b, L0_ffn_w1, L0_ffn_b1, L0_ffn_w2, L0_ffn_b2))
    x = x + s * g
    xn = _layernorm(x, axis=-1)
    s = _L1_attn_ref(xn, L1_attn_wq, L1_attn_bq, L1_attn_wqc, L1_attn_bqc, L1_attn_wqr, L1_attn_bqr, L1_attn_wkv, L1_attn_bkv, L1_attn_wkr, L1_attn_bkr, L1_attn_wkc, L1_attn_bkc, L1_attn_wv, L1_attn_bv, L1_attn_wo, L1_attn_bo)
    g = _silu(_L1_ffn_ref(xn, L1_ffn_w_q, L1_ffn_bn_gamma, L1_ffn_bn_beta, L1_ffn_keys, L1_ffn_down_embed, L1_ffn_up_embed))
    x = x + s * g
    xn = _layernorm(x, axis=-1)
    s = _L2_attn_ref(xn, L2_attn_W, L2_attn_proj, L2_attn_concat_w, L2_attn_concat_b)
    g = _silu(_L2_ffn_ref(xn, L2_ffn_weight))
    x = x + s * g
    xn = _layernorm(x, axis=-1)
    s = _L3_attn_ref(xn, L3_attn_w_qkv, L3_attn_w_proj, L3_attn_b_proj, L3_attn_lambda_q1, L3_attn_lambda_k1, L3_attn_lambda_q2, L3_attn_lambda_k2, L3_attn_sub_norm_w)
    g = _silu(_L3_ffn_ref(xn, L3_ffn_Wr, L3_ffn_W1, L3_ffn_b1, L3_ffn_W2, L3_ffn_b2))
    x = x + s * g
    return x

_drawn_inputs = setup_inputs


def setup_inputs(seed=0):
    import zlib

    import numpy as np

    out = dict(_drawn_inputs(seed))
    spreads = {'L0_ffn_q_scale': (1.0, 0.6),
     'L0_ffn_k_scale': (1.0, 0.6),
     'L0_ffn_ln_g': (1.0, 0.6),
     'L0_ffn_ln_b': (0.0, 0.8),
     'L0_ffn_b1': (0.0, 0.8),
     'L0_ffn_b2': (0.0, 0.321),
     'L1_ffn_bn_gamma': (1.0, 0.6),
     'L1_ffn_bn_beta': (0.0, 0.8),
     'L2_attn_concat_b': (0.0, 0.1),
     'L3_attn_b_proj': (0.0, 0.8),
     'L3_attn_sub_norm_w': (1.0, 0.6)}
    factors = {'L0_ffn_wqkv': 8.0,
     'L0_ffn_wo': 7.817,
     'L0_ffn_w1': 8.0,
     'L0_ffn_w2': 8.0,
     'L1_attn_wqr': 8.0,
     'L1_attn_bqr': 8.0,
     'L1_attn_wkv': 8.0,
     'L1_attn_bkv': 8.0,
     'L1_attn_wkr': 8.0,
     'L1_attn_bkr': 8.0,
     'L1_attn_wv': 8.0,
     'L1_attn_bv': 8.0,
     'L1_attn_wo': 8.0,
     'L1_attn_bo': 23.768,
     'L1_ffn_w_q': 8.0,
     'L1_ffn_keys': 8.0,
     'L1_ffn_down_embed': 8.0,
     'L1_ffn_up_embed': 8.0,
     'L3_attn_w_qkv': 8.0,
     'L3_attn_w_proj': 8.0,
     'L3_attn_lambda_q1': 200.0,
     'L3_attn_lambda_k1': 200.0,
     'L3_attn_lambda_q2': 8.0,
     'L3_attn_lambda_k2': 8.0,
     'L3_ffn_Wr': 8.0,
     'L3_ffn_W1': 8.0,
     'L3_ffn_b1': 200.0,
     'L3_ffn_W2': 8.0,
     'L3_ffn_b2': 200.0}
    for name, (base, spread) in spreads.items():
        noise = np.random.default_rng([zlib.crc32(name.encode()), seed]).standard_normal(out[name].shape)
        drawn = base * np.exp(spread * noise) if base else spread * noise
        out[name] = jnp.asarray(drawn.astype(out[name].dtype))
    for name, factor in factors.items():
        out[name] = (out[name] * factor).astype(out[name].dtype)
    return out
```

```python
from contextlib import ExitStack

import numpy as np

import concourse.bass as bass
from concourse import mybir

P = 128
BATCH, SEQ = 2, 1024
TOK = BATCH * SEQ
TILES = TOK // P
QT = SEQ // P
BL = 512
BLOCKS = TOK // BL
SB = SEQ // BL
D = 128
EPS = 1e-5

F32 = mybir.dt.float32
BF16 = mybir.dt.bfloat16
U32 = mybir.dt.uint32
ALU = mybir.AluOpType
ACT = mybir.ActivationFunctionType
AX_X = mybir.AxisListType.X

DEPTH, FH, FD = 2, 8, 64
HID = int(D * 4 * 2 / 3)
HCH = -(-HID // P)
HROWS = [min(P, HID - P * c) for c in range(HCH)]
PH, NK, TOPK = 8, 32, 8
EXPCH = NK * NK // P
E3, M3 = 8, 512
LAMBDA_INIT = 0.8 - 0.6 * float(np.exp(-0.3 * 0))
GONE = -3.0e38

Q_PART = [0, 0, 0, 1, 1, 2]
K_PART = [0, 1, 2, 0, 1, 0]
SLOTS = 3


class Event:

    def __init__(self, sem, base):
        self.sem, self.base = sem, base

    def __call__(self, k):
        assert self.base + k > 0
        return self.sem, self.base + k


class Attention:

    def __init__(self, name, heads, chunk, width, split, window, causal, scale, halves=1, batches=BATCH):
        self.name, self.width, self.split, self.scale = name, width, split, scale
        self.window, self.causal, self.halves = window, causal, halves
        self.chunk = chunk
        self.rows = width * 6 if split else width
        self.max_at = chunk * self.rows
        self.heads = heads
        self.chunks = heads // chunk
        self.vrows = 32 if self.split else 64
        self.perbank = P // self.vrows
        self.batches = batches
        self.groups = 4
        self.steps = batches * self.groups
        self.a_units = self.first_pass()
        self.ring = len(self.a_units) + 2
        self.b_quads = self.second_pass()
        self.quads = len(self.b_quads)
        self.fills = halves * SB
        self.total = self.quads * self.perbank
        pace = 0.93 if halves == 2 else 0.65 if window and split else 0.84 if window else 0.8
        self.logit_banks, self.sum_banks = ([4, 5, 7], [6]) if halves == 2 else ([4, 5], [6, 7] if split else [6])
        self.sent_at = [int(k * pace * self.total / self.ring) for k in range(self.ring)]

    def first_pass(self):
        out = []
        for qt in range(QT):
            k1 = (qt + 1) * P if self.causal else SEQ
            k0 = max(qt - 1, 0) * P if self.window else 0
            wide = next(s for s in (256, 512, 1024) if k1 - k0 <= s)
            n = min(self.heads, 1024 // wide)
            out += [(qt, h, n, wide, k0, k1) for h in range(0, self.heads, n)]
        return out

    def second_pass(self):
        out = []
        for half in range(self.halves):
            for qb in range(SB):
                base = qb * BL
                packs = []
                for kt in range(QT):
                    q0 = max(kt * P - base, 0) if self.causal else 0
                    q1 = min(kt * P + 2 * P - base, BL) if self.window else BL
                    if q0 >= q1:
                        continue
                    for p in packs:
                        used = sum(s[2] - s[1] for s in p)
                        if used + q1 - q0 <= BL:
                            p.append((kt, q0, q1, used))
                            break
                    else:
                        packs.append([(kt, q0, q1, 0)])
                out += [(half, qb, p, i == 0, i == len(packs) - 1) for i, p in enumerate(packs)]
        return out


STAGES = ["load", "ln0", "a0_prep", "a0", "a0_post"]
for _l in range(DEPTH):
    for _b in range(BATCH):
        STAGES += [f"f0_prep{_l}{_b}", f"f0_att{_l}{_b}", f"f0_out{_l}{_b}"]
    STAGES += [f"f0_mlp{_l}"]
STAGES += ["gate0", "ln1", "a1_prep", "a1", "a1_post", "f1_q", "f1_tm", "gate1", "ln2", "f2", "gate2",
           "ln3", "a3_prep", "a3", "a3_post", "f3", "gate3", "store"]
COMPUTE = 3


def build(nc, w, out):
    with ExitStack() as ctx:
        def sb(name, shape, dt=F32):
            return ctx.enter_context(nc.sbuf_tensor(name, shape, dt))

        sems, counted = {}, {}

        def event(name, n):
            if name not in sems:
                sems[name] = ctx.enter_context(nc.semaphore(name))
                counted[name] = 0
            e = Event(sems[name], counted[name])
            counted[name] += n
            return e

        def Events(prefix, **counts):
            return {n: event(prefix + n, c) for n, c in counts.items()}

        psum = ctx.enter_context(nc.psum_tensor("psum", [P, 8 * BL], F32))
        bank = [psum[:, i * BL:(i + 1) * BL] for i in range(8)]
        score_ring = [psum[:, 0:2 * BL], psum[:, 2 * BL:4 * BL]]

        xT, xnT, sT, hT = sb("xT", [P, TOK]), sb("xnT", [P, TOK]), sb("sT", [P, TOK]), sb("hT", [P, TOK])
        zT = hT
        ones, mean_of, eps = sb("ones", [P, P]), sb("mean_of", [P, P]), sb("eps", [P, 1])
        small = sb("small", [P, 64])
        m_tm = sb("m_tm", [P, 2, QT, 8])
        mT = sb("mT", [P, 2, SEQ], BF16)
        R = {}
        groups = {}

        def load(group, *names):
            groups[group] = names

        load("consts", "ident", "identb", "masks", "blk64", "blk32", "denrow", "selp", "iota", "iota_ka", "rankw")
        for name in groups["consts"]:
            held = sb("w_" + name, list(w[name].shape), w[name].dtype)
            R[name] = held[tuple(slice(None) for _ in w[name].shape)]

        ARENA = 41984
        arena = sb("arena", [P, ARENA])

        class Carver:

            def __init__(self, at=0):
                self.at = at

            def f32(self, n):
                assert self.at + n <= ARENA, (self.at, n)
                self.at += n
                return arena[:, self.at - n:self.at]

            def bf16(self, n):
                return self.f32(n // 2).bitcast(BF16)

            def weights(self, group, *names):
                load(group, *names)
                for name in names:
                    s = w[name].shape
                    n = int(np.prod(s[1:]))
                    v = self.f32(n)[0:s[0], :]
                    if len(s) == 3:
                        v = v.rearrange("p (a b) -> p a b", a=s[1])
                    if len(s) == 4:
                        v = v.rearrange("p (a b c) -> p a b c", a=s[1], b=s[2])
                    R[name] = v

        def att_buffers(c, a):
            class B:
                pass
            b = B()
            if a.split:
                K = c.bf16(SLOTS * a.chunks * a.chunk * SEQ).rearrange("p (s c a t) -> p s c a t", s=SLOTS, c=a.chunks, a=a.chunk)
                Q = c.bf16(SLOTS * a.chunks * SEQ).rearrange("p (s c t) -> p s c t", s=SLOTS, c=a.chunks)
                b.K, b.Q = (lambda s: K[:, s % SLOTS]), (lambda s: Q[:, s % SLOTS])
                b.kall, b.qall = K, Q
            else:
                K = c.f32(a.groups * a.chunk * SEQ).rearrange("p (s c a t) -> p s c a t", s=a.groups, c=1, a=a.chunk)
                Q = c.f32(a.groups * SEQ).rearrange("p (s c t) -> p s c t", s=a.groups, c=1)
                b.K, b.Q = (lambda s: K[:, s]), (lambda s: Q[:, s])
                b.kall, b.qall = K, Q
                b.logden = c.f32(a.groups * SEQ).rearrange("p (g t) -> p g t", g=a.groups)
            b.V = c.f32(SLOTS * QT * P).rearrange("p (s t n) -> p s t n", s=SLOTS, t=QT)
            b.PT = c.f32(8 * BL).rearrange("p (s n) -> p s n", s=8)
            n = a.halves * a.groups * a.batches * SEQ
            b.o = c.f32(n).rearrange("p (h g t) -> p h g t", h=a.halves, g=a.groups)
            return b

        A0 = Attention("a0", 4, 2, 8, True, True, True, 8 ** -0.5)
        F0 = Attention("f0", 2, 2, FD, False, True, True, 8.0, batches=1)
        A1 = Attention("a1", 4, 2, 8, True, False, True, 8 ** -0.5)
        A3 = Attention("a3", 8, 4, 4, True, False, False, 4 ** -0.5, halves=2)

        c = Carver()
        u1, u2, u3 = c.f32(TOK), c.f32(TOK), c.f32(TOK)
        c.weights("x", "x_tm")

        c = Carver()
        c.weights("a0", "a0_qk", "a0_wv", "a0_wo", "a0_cos", "a0_sin")
        B0 = att_buffers(c, A0)
        c.at -= B0.o.shape[1] * B0.o.shape[2] * B0.o.shape[3] + 8 * BL
        prep_at = c.at

        def prep_buffers(at):
            c = Carver(at)
            return (c.f32(2 * BL).rearrange("p (x t) -> p x t", x=2), c.f32(2 * BL).rearrange("p (x t) -> p x t", x=2),
                    c.f32(2 * BL).rearrange("p (x t) -> p x t", x=2),
                    c.bf16(3 * 2 * TOK).rearrange("p (x r t) -> p x r t", x=2, r=3))
        PB0 = prep_buffers(prep_at)
        FW = []
        for l in range(DEPTH):
            c = Carver()
            c.weights(f"f0{l}", *(f"f0_{n}{l}" for n in ("qk", "wv", "wo", "w1", "w2", "vec", "b1")))
            if l == 0:
                c.weights("f0_tables", "f0_tab")
            else:
                c.f32(4 * SEQ)
        BF = att_buffers(c, F0)
        fa, fb, fc, fd = (c.f32(2 * BL).rearrange("p (x t) -> p x t", x=2) for _ in range(4))
        spent = BF.logden.rearrange("p g (n t) -> p (g n) t", t=BL)
        hid, gel = spent[:, 0:3], spent[:, 3:6]
        c = Carver()
        c.weights("a1", "a1_qk", "a1_b", "a1_wkv", "a1_bkv", "a1_wv", "a1_wo", "a1_cos", "a1_sin")
        ckv = c.f32(TOK)
        B1 = att_buffers(c, A1)
        PB1 = prep_buffers(c.at - B1.o.shape[1] * B1.o.shape[2] * B1.o.shape[3] - 8 * BL)
        c = Carver()
        c.weights("a3", "a3_qk", "a3_wv", "a3_wo", "a3_vec", "a3_lam")
        B3 = att_buffers(c, A3)
        PB3 = prep_buffers(c.at - 4 * TOK * 2 - 8 * BL)
        c = Carver()
        c.weights("f1", "f1_wq", "f1_gb", "f1_keys", "f1_down", "f1_up")
        simT = c.f32(4 * TOK).rearrange("p (g t) -> p g t", g=4)
        at_f1 = c.at
        qn = c.f32(2 * TOK).rearrange("p (s t) -> p s t", s=2)
        bnst = c.f32(16 * 24).rearrange("p (c n) -> p c n", c=16)
        bnmv = c.f32(32).rearrange("p (c n) -> p c n", c=16)
        bnx = c.f32(64).rearrange("p (k c) -> p k c", k=4)
        c = Carver(at_f1)
        sim = c.f32(2 * 512).rearrange("p (s h x k) -> p s h x k", s=2, h=PH, x=2)
        comb = c.f32(512).rearrange("p (h n) -> p h n", h=PH)
        rep = c.f32(512).rearrange("p (h n) -> p h n", h=PH)
        top = c.f32(128).rearrange("p (h x a) -> p h x a", h=PH, x=2)
        idx = c.f32(128).bitcast(U32).rearrange("p (h x a) -> p h x a", h=PH, x=2)
        idxf = c.bf16(128).rearrange("p (x n) -> p x n", x=2)
        sc8 = c.f32(64).rearrange("p (h a) -> p h a", h=PH)
        es8 = c.f32(64).rearrange("p (h a) -> p h a", h=PH)
        nsel = c.f32(64)
        zr = c.f32(32).rearrange("p (k h) -> p k h", k=4)
        exy = c.f32(2 * 512).rearrange("p (s x h k) -> p s x h k", s=2, x=2, h=PH)
        nselb = c.bf16(64)
        below = c.bf16(256).rearrange("p (h k) -> p h k", h=PH)
        rank = c.f32(512).rearrange("p (x h k) -> p x h k", x=2, h=PH)
        onehot = c.bf16(2048).rearrange("p (h k a) -> p h k a", h=PH, k=NK)
        rows_of = c.bf16(2 * 1024).rearrange("p (s e) -> p s e", s=2)
        pairs = c.bf16(2 * 1024).rearrange("p (s e) -> p s e", s=2)
        dm = c.f32(8 * 1024).rearrange("p (s e) -> p s e", s=8)
        Wd = c.f32(2 * 1024).rearrange("p (s e) -> p s e", s=2)
        gd = c.f32(2 * 1024).rearrange("p (s e) -> p s e", s=2)
        hwT = c.f32(1024).rearrange("p (c t) -> p c t", c=EXPCH)
        c = Carver()
        c.weights("f2", "f2_w")
        signs = c.f32(P)
        c = Carver()
        c.weights("f3", "f3_wr", "f3_w1", "f3_b1", "f3_w2", "f3_b2", "f3_selw")
        g3 = c.f32(4 * BL).rearrange("p (s t) -> p s t", s=4)
        gw3 = c.f32(4 * BL).rearrange("p (s t) -> p s t", s=4)
        wT3 = c.f32(TOK)
        r3 = [c.f32(TILES * E3).rearrange("p (t e) -> p t e", t=TILES) for _ in range(9)]
        v3 = [c.f32(TILES) for _ in range(5)]

        scratch = nc.dram_tensor("parts", (2, 3, P, TOK), BF16, kind="Internal").ap()

        stage_done = event("stage_done", 0).sem
        load_done = {g: event("loaded_" + ("x" if g == "x" else "weights"), 16 * len(groups[g])) for g in
                     ("x", "consts", "a0", "f0_tables", "f00", "f01", "a1", "f1", "f2", "a3", "f3")}
        LOADS = {"a0": "a0_prep", "f00": "f0_prep00", "f01": "f0_prep10", "a1": "a1_prep", "f1": "f1_q", "f2": "f2",
                 "a3": "a3_prep", "f3": "f3"}

        def weights_in(eng, g):
            eng.wait_ge(*load_done[g](16 * len(groups[g])))

        IO = Events("io_", turned=4, x=4, back=4, out=4, stored=4 * 16)
        LN = [None] * 4

        def ln_events(i):
            LN[i] = Events("ln_", mean=4, cent=4, sq=4, var=4, log=4, rstd=4, out=4)

        ln_events(0)
        GATE = [Events("gate_", silu=1, mix=1, x=1) for _ in range(4)]

        def prep_events(rotated=True, gelu=False):
            n, m = 8 * rotated, 8 * gelu
            return Events("prep_", proj=8, rc=n, rs=n, raw=8, gelu=m, hi=8, r1=8, mid=8, lo=8, ckv=m // 2, ckvo=m // 2)

        def att_events(a):
            e = Events("att_", scored=a.steps * a.ring, maxed=a.steps * a.ring, high=a.steps,
                       logits=a.steps * a.quads * a.perbank, probs=a.steps * a.quads * a.perbank,
                       summed=a.steps * a.quads, taken=a.steps * a.fills * (1 if a.split else 2),
                       zeroed=0, ones=0, parts=0, kq=0, rows=0)
            if a.split:
                e["zeroed"] = event("att_zeroed", 1)
                e["ones"], e["parts"] = event("att_ones", 16 * SLOTS * a.chunk), event("att_parts", 16 * 12)
                e["per"] = 16 * 6 * (1 + a.chunk)
                e["kq"] = [event(f"att_kq{k}", len(range(k, a.steps, SLOTS)) * e["per"]) for k in range(SLOTS)]
                e["rows"] = event("att_rows", a.steps * 16 * 2 * a.chunks)
            return e

        def post_events(a):
            n = BLOCKS * 4 * a.halves
            m = 16 * (a.halves == 2)
            return Events("post_", den=n, log=n, inv=n, norm=n, od=m, sq=m, ms=m, log2=m, rstd=m, on=m,
                          out=BLOCKS, s=BLOCKS)

        PREP, ATT, POST = {}, {}, {}
        PREP["a0"], ATT["a0"], POST["a0"] = prep_events(), att_events(A0), post_events(A0)
        FS, FMS, FP, FA, FO, FM, LNF = [], [], {}, {}, {}, [], []
        for l in range(DEPTH):
            FS.append(Events("fshift_", h=3))
            for b in range(BATCH):
                FP[l, b] = Events("fprep_", proj=16, rot=16, sq=16, nrm=16, clamp=16, log=16, inv=16, qc=16, qr=16,
                                  sum=16, out=24)
                FA[l, b] = att_events(F0)
                if (l, b) == (0, 0):
                    FA[l, b]["zeroed"] = event("att_zeroed", 1)
                FO[l, b] = Events("fout_", inv=4, norm=4, o=2, y=2)
            FMS.append(Events("fshift_", h=3))
            LNF.append(Events("ln_", mean=4, cent=4, sq=4, var=4, log=4, rstd=4))
            FM.append(Events("fmlp_", norm=4, xh=4, g=12, a=12, gelu=12,
                             hid=12, down=4, y=4))
        ln_events(1)
        PREP["a1"], ATT["a1"], POST["a1"] = prep_events(gelu=True), att_events(A1), post_events(A1)
        PQ = Events("pq_", q=64, st=64, mv=16, log=16, rstd=16, sc=16, tmp=16, sh=16, qn=64, sim=16, simT=16)
        PK = Events("pick_", turn=16, tm=16, top=256, idx=256, idxf=32, comb=16, sc8=128, rep=128, mask=16, nsel=16,
                    sub8=16, e8=16, z=16, rz=16, sub=32, exy=32, exz=16, eq=32, wt=32, rank=32, below=16, nselb=16, spread=128, m=128, me=128,
                    w=16 * 7, acc=128, hd=32, gd=32, hw=16, wt2=32, hwT=32, out=16, z2=16)
        ln_events(2)
        F2 = Events("f2_", signs=1, z=4, out=4)
        ln_events(3)
        PREP["a3"], ATT["a3"], POST["a3"] = prep_events(rotated=False), att_events(A3), post_events(A3)
        LAM = Events("lam_", weight=1, prod=1, sum=1, exp=1, part=1, neg=1)
        MO = Events("pick_", logit=1, max=1, sub=1, exp=1, sum=1, inv=1, prob=1, top=16, idx=16, idxf=1, den=1, rden=1,
                    o0=1, o1=1, m0=1, m1=1, w=1, wn=1, turn=4, wT=4, wb=32, h=128, gelu=128, gw=128, out=4, z=4)
        POOLED = event("pool_step", 3)
        POOLED.n = 0
        counted_events = len(sems)
        assert counted_events <= 156, counted_events

        block = ctx.enter_context(nc.Block())

        def barrier(eng, name):
            n = STAGES.index(name) + 1
            eng.drain().then_inc(stage_done, 1)
            eng.wait_ge(stage_done, COMPUTE * n)

        def after(eng, name):
            eng.wait_ge(stage_done, COMPUTE * (STAGES.index(name) + 1))

        def before(name):
            return STAGES[STAGES.index(name) - 1]

        @block.sync
        def _(sp):
            def fetch(g):
                for name in groups[g]:
                    sp.dma_start(R[name], w[name]).then_inc(load_done[g].sem, 16)

            def attention(a, e, B):
                G, W = a.chunk, a.width
                pr = PREP[a.name]
                parts = (PB0, PB1, PB3)[("a0", "a1", "a3").index(a.name)][3]

                def spill(b):
                    sp.wait_ge(*pr["lo"](2 * SB * (b + 1)))
                    for x in range(2):
                        for r in range(3):
                            t = slice(b * SEQ, (b + 1) * SEQ)
                            sp.dma_start(scratch[x, r, :, t], parts[:, x, r, t]).then_inc(e["parts"].sem, 16)

                spill(0)
                sp.wait_ge(*e["zeroed"](1))
                for s in range(SLOTS):
                    for g in range(G):
                        r = slice(a.max_at + g, a.max_at + 2 * G, G)
                        sp.dma_start(B.kall[r, s, :, g, :], w["one_rows"]).then_inc(e["ones"].sem, 16)
                sp.wait_ge(*e["parts"](16 * 6))

                def fill(s):
                    b, g4 = divmod(s, a.groups)
                    if s >= SLOTS:
                        sp.wait_ge(*e["summed"]((s - SLOTS + 1) * a.quads))
                    if s == a.groups:
                        sp.wait_ge(*e["parts"](16 * 12))
                    rows = slice(g4 * a.heads * W, (g4 + 1) * a.heads * W)
                    for x, part in enumerate((Q_PART, K_PART)):
                        src = scratch[x, :, rows, b * SEQ:(b + 1) * SEQ]
                        for i, p in enumerate(part):
                            at = i * G * W
                            if x == 0:
                                sp.dma_start(B.Q(s)[at:at + G * W], src[p].rearrange("(c r) t -> r c t", r=G * W)) \
                                  .then_inc(e["kq"][s % SLOTS].sem, 16)
                            else:
                                heads = src[p].rearrange("(c a d) t -> a d c t", a=G, d=W)
                                for g in range(G):
                                    sp.dma_start(B.K(s)[at + g * W:at + (g + 1) * W, :, g, :], heads[g]) \
                                      .then_inc(e["kq"][s % SLOTS].sem, 16)

                def max_rows(s):
                    sp.wait_ge(*e["maxed"]((s + 1) * a.ring))
                    for c in range(a.chunks):
                        for k in range(2):
                            r = a.max_at + k * G
                            sp.dma_start(B.Q(s)[r:r + G, c, :], mT[32 * k + c * G:32 * k + (c + 1) * G, s % 2, :]) \
                              .then_inc(e["rows"].sem, 16)

                fill(0)
                spill(1)
                for s in range(1, SLOTS):
                    fill(s)
                for s in range(a.steps):
                    max_rows(s)
                    if s >= 1 and s + SLOTS - 1 < a.steps:
                        fill(s + SLOTS - 1)

            fetch("x")
            fetch("consts")
            after(sp, before(LOADS["a0"]))
            fetch("a0")
            attention(A0, ATT["a0"], B0)
            after(sp, before(LOADS["f00"]))
            fetch("f0_tables")
            for g in ("f00", "f01", "a1"):
                after(sp, before(LOADS[g]))
                fetch(g)
            attention(A1, ATT["a1"], B1)
            for g in ("f1", "f2", "a3"):
                after(sp, before(LOADS[g]))
                fetch(g)
            attention(A3, ATT["a3"], B3)
            after(sp, before(LOADS["f3"]))
            fetch("f3")
            res = out.rearrange("b (n p) d -> p (b n) d", p=P)
            for n in range(BLOCKS):
                sp.wait_ge(*IO["out"](n + 1))
                sp.dma_start(res[:, 4 * n:4 * n + 4, :], u1[:, n * BL:(n + 1) * BL].rearrange("p (n d) -> p n d", d=D)) \
                  .then_inc(IO["stored"].sem, 16)
            sp.wait_ge(*IO["stored"](16 * BLOCKS))

        def blk(n):
            return slice(n * BL, (n + 1) * BL)

        def unit_events(a):
            return [(s, k) for s in range(a.steps) for k in range(a.ring)]

        @block.tensor
        def _(pe):
            def layer_norm(e):
                for n in range(BLOCKS):
                    pe.matmul(bank[n], mean_of[:, :], xT[:, blk(n)], start=True, stop=True).then_inc(e["mean"].sem, 1)
                for n in range(BLOCKS):
                    pe.wait_ge(*e["sq"](n + 1))
                    pe.matmul(bank[4 + n], mean_of[:, :], u2[:, blk(n)], start=True, stop=True).then_inc(e["var"].sem, 1)

            def attention(a, e, B, vsrc, vrows, wv, t0=0):
                def ring_use(s, k):
                    r = s * a.ring + k
                    if r >= 2:
                        pe.wait_ge(*e["maxed"](r - 1))
                    dst = score_ring[r % 2]
                    b, g = divmod(s, a.groups)
                    if k == 0:
                        wide = P if a.split else a.heads * a.vrows
                        at = 0 if a.split else g * wide
                        for t in range(QT):
                            tok = t0 + (b * QT + t) * P
                            mm = pe.matmul(dst[:, t * P:(t + 1) * P], vsrc[0:vrows, tok:tok + P], wv[0:vrows, at:at + P],
                                           start=True, stop=True)
                        mm.then_inc(e["scored"].sem, 1)
                        return
                    K, Q = B.K(s), B.Q(s)
                    if k == a.ring - 1:
                        pe.wait_ge(*e["maxed"](r))
                        for q in range(QT):
                            mm = pe.transpose(dst[0:a.heads, q * P:(q + 1) * P], m_tm[:, s % 2, q, 0:a.heads], R["ident"][:, :])
                        mm.then_inc(e["scored"].sem, 1)
                        return
                    if k == 1 and a.split:
                        pe.wait_ge(*e["kq"][s % SLOTS]((s // SLOTS + 1) * e["per"]))
                        if s == 0:
                            pe.wait_ge(*e["ones"](16 * SLOTS * a.chunk))
                            pe.wait_ge(*e["parts"](16 * 12))
                    qt, h0, n, wide, k0, k1 = a.a_units[k - 1]
                    for i in range(n):
                        c, g = divmod(h0 + i, a.chunk)
                        for x0 in range(k0, k1, BL):
                            x1 = min(x0 + BL, k1)
                            mm = pe.matmul(dst[:, i * wide + x0 - k0:i * wide + x1 - k0], Q[0:a.max_at, c, qt * P:(qt + 1) * P],
                                           K[0:a.max_at, c, g, x0:x1], start=True, stop=not (a.causal and x1 == k1),
                                           skip_group_check=True)
                        if a.causal:
                            end = i * wide + k1 - k0
                            if a.window and qt:
                                pe.matmul(dst[:, i * wide:i * wide + P], R["identb"][:, :], R["masks"][:, 1, :],
                                          start=False, stop=False, skip_group_check=True)
                            mm = pe.matmul(dst[:, end - P:end], R["identb"][:, :], R["masks"][:, 0 if a.window else 2, :],
                                           start=False, stop=True, skip_group_check=True)
                    mm.then_inc(e["scored"].sem, 1)

                def logits(s, q, j):
                    half, qb, segs, first, last = a.b_quads[q]
                    n = (s * a.quads + q) * a.perbank + j
                    h = a.halves * j + half
                    c, g = divmod(h, a.chunk)
                    if q == 0 and j == 0:
                        if a.split:
                            pe.wait_ge(*e["rows"]((s + 1) * 16 * 2 * a.chunks))
                        else:
                            pe.wait_ge(*e["maxed"]((s + 1) * a.ring))
                    depth = len(a.logit_banks)
                    if n >= depth:
                        pe.wait_ge(*e["probs"](n - depth + 1))
                    dst = bank[a.logit_banks[n % depth]]
                    K, Q = B.K(s), B.Q(s)
                    for kt, q0, q1, at in segs:
                        base = qb * BL
                        diag = a.causal and kt * P - base >= 0
                        off = a.window and (kt + 1) * P - base < q1
                        steps = [diag, off, not a.split]
                        mm = pe.matmul(dst[:, at:at + q1 - q0], K[:, c, g, kt * P:(kt + 1) * P], Q[:, c, base + q0:base + q1],
                                       start=True, stop=not any(steps), skip_group_check=True)
                        if diag:
                            mm = pe.matmul(dst[:, at:at + P], R["identb"][:, :], R["masks"][:, 3 if a.window else 5, :],
                                           start=False, stop=not any(steps[1:]), skip_group_check=True)
                        if off:
                            x = at + (kt + 1) * P - base - q0
                            mm = pe.matmul(dst[:, x:x + P], R["identb"][:, :], R["masks"][:, 4, :],
                                           start=False, stop=not steps[2], skip_group_check=True)
                        if not a.split:
                            mm = pe.matmul(dst[:, at:at + q1 - q0], R["selp"][:, h, :], mT[:, s % 2, base + q0:base + q1],
                                           start=False, stop=True, skip_group_check=True)
                    mm.then_inc(e["logits"].sem, 1)

                def weigh(s, q):
                    half, qb, segs, first, last = a.b_quads[q]
                    n = s * a.quads + q
                    f = s * a.fills + half * SB + qb
                    pe.wait_ge(*e["probs"]((n + 1) * a.perbank))
                    if first:
                        if a.split and f >= len(a.sum_banks):
                            pe.wait_ge(*e["taken"](f - len(a.sum_banks) + 1))
                        if not a.split and f >= 1:
                            pe.wait_ge(*e["taken"](2 * f))
                    for i, (kt, q0, q1, at) in enumerate(segs):
                        for j in range(a.perbank):
                            r = slice(j * a.vrows, (j + 1) * a.vrows)
                            p = B.PT[:, (n * a.perbank + j) % 8, at:at + q1 - q0]
                            dst = bank[a.sum_banks[f % len(a.sum_banks)]]
                            st, sp_ = first and i == 0, last and i == len(segs) - 1
                            mm = pe.matmul(dst[r, q0:q1], B.V[:, s % SLOTS, kt, r], p, start=st, stop=sp_, skip_group_check=True)
                            if not a.split:
                                mm = pe.matmul(bank[7][r, q0:q1], ones[:, 0:a.vrows], p, start=st, stop=sp_,
                                               skip_group_check=True)
                    mm.then_inc(e["summed"].sem, 1)

                for k in range(a.ring):
                    ring_use(0, k)
                for s in range(a.steps):
                    for i in range(a.total):
                        q, j = divmod(i, a.perbank)
                        logits(s, q, j)
                        if s + 1 < a.steps:
                            for k in range(a.ring):
                                if a.sent_at[k] == i:
                                    ring_use(s + 1, k)
                        if q >= 1 and j == min(1, a.perbank - 1):
                            weigh(s, q - 1)
                    weigh(s, a.quads - 1)

            def post(a, e, B, wo):
                i = 0
                for n in range(BLOCKS):
                    for hg in range(a.halves * 4):
                        h, g = divmod(hg, 4)
                        if i >= 2:
                            pe.wait_ge(*e["log"](i - 1))
                        pe.matmul(bank[i % 2], R["denrow"][:, :], B.o[:, h, g, blk(n)], start=True, stop=True) \
                          .then_inc(e["den"].sem, 1)
                        i += 1
                for n in range(BLOCKS):
                    if a.halves == 2:
                        for g in range(4):
                            k = 4 * n + g
                            pe.wait_ge(*e["sq"](k + 1))
                            if k >= 2:
                                pe.wait_ge(*e["log2"](k - 1))
                            pe.matmul(bank[4 + k % 2], R["blk32"][:, :], B.o[:, 1, g, blk(n)], start=True, stop=True) \
                              .then_inc(e["ms"].sem, 1)
                        pe.wait_ge(*e["on"](4 * n + 4))
                    else:
                        pe.wait_ge(*e["norm"](4 * n + 4))
                    if n >= 2:
                        pe.wait_ge(*e["s"](n - 1))
                    for g in range(4):
                        mm = pe.matmul(bank[2 + n % 2], wo[:, g, :], B.o[:, 0, g, blk(n)], start=(g == 0), stop=(g == 3))
                    mm.then_inc(e["out"].sem, 1)

            weights_in(pe, "x")
            weights_in(pe, "consts")
            for n in range(BLOCKS):
                for t in range(4):
                    mm = pe.transpose(bank[n][:, t * P:(t + 1) * P], R["x_tm"][:, 4 * n + t, :], R["ident"][:, :])
                mm.then_inc(IO["turned"].sem, 1)
            barrier(pe, "load")
            layer_norm(LN[0])
            barrier(pe, "ln0")

            def projections(e, wqk, nproj):
                per = nproj // 2
                for n in range(BLOCKS):
                    for x in range(2):
                        if n >= 2:
                            pe.wait_ge(*e["raw"](2 * (n - 2) + x + 1))
                        for c in range(per):
                            mm = pe.matmul(bank[(n % 2) * 4 + 2 * x + c], wqk[:, x * per + c, :], xnT[:, blk(n)], start=True, stop=True)
                        mm.then_inc(e["proj"].sem, 1)

            weights_in(pe, "a0")
            projections(PREP["a0"], R["a0_qk"], 4)
            barrier(pe, "a0_prep")
            attention(A0, ATT["a0"], B0, xnT, P, R["a0_wv"])
            barrier(pe, "a0")
            post(A0, POST["a0"], B0, R["a0_wo"])
            barrier(pe, "a0_post")

            def norms(e, i):
                pe.wait_ge(*e["sq"](i + 1))
                if i >= 2:
                    pe.wait_ge(*e["clamp"](i - 1))
                pe.matmul(bank[4 + i % 2], R["blk64"][:, :], fa[:, i % 2, :], start=True, stop=True).then_inc(e["nrm"].sem, 1)

            for l in range(DEPTH):
                for b in range(BATCH):
                    e = FP[l, b]
                    weights_in(pe, f"f0{l}")
                    if b == 0:
                        pe.wait_ge(*FS[l]["h"](3))
                    for i in range(16):
                        x, c, n = i // 8, i // 2 % 4, i % 2
                        s = slice(b * SEQ + n * BL, b * SEQ + (n + 1) * BL)
                        if i >= 2:
                            pe.wait_ge(*e["qc"](i - 1))
                            pe.wait_ge(*e["sq"](i - 1))
                        pe.matmul(bank[i % 2], R[f"f0_qk{l}"][:, 2 * x, c * P:(c + 1) * P], hT[:, s],
                                  start=True, stop=True).then_inc(e["proj"].sem, 1)
                        if i >= 2:
                            pe.wait_ge(*e["qr"](i - 1))
                        pe.matmul(bank[2 + i % 2], R[f"f0_qk{l}"][:, 2 * x + 1, c * P:(c + 1) * P], hT[:, s],
                                  start=True, stop=True).then_inc(e["rot"].sem, 1)
                        if i >= 1:
                            norms(e, i - 1)
                    norms(e, 15)
                    barrier(pe, f"f0_prep{l}{b}")
                    attention(F0, FA[l, b], BF, hT, P, R[f"f0_wv{l}"], t0=b * SEQ)
                    barrier(pe, f"f0_att{l}{b}")
                    e = FO[l, b]
                    for n in range(SB):
                        for g in range(4):
                            pe.wait_ge(*e["norm"](g + 1))
                            mm = pe.matmul(bank[n], R[f"f0_wo{l}"][:, g, :], BF.o[:, 0, g, blk(n)], start=(g == 0), stop=(g == 3))
                        mm.then_inc(e["o"].sem, 1)
                    barrier(pe, f"f0_out{l}{b}")
                f = FM[l]
                for n in range(BLOCKS):
                    pe.wait_ge(*FMS[l]["h"](3))
                    pe.matmul(bank[n], mean_of[:, :], hT[:, blk(n)], start=True, stop=True).then_inc(LNF[l]["mean"].sem, 1)
                for n in range(BLOCKS):
                    pe.wait_ge(*LNF[l]["sq"](n + 1))
                    pe.matmul(bank[4 + n], mean_of[:, :], BF.PT[:, 4 + n, :], start=True, stop=True).then_inc(LNF[l]["var"].sem, 1)
                pe.wait_ge(*LNF[l]["log"](BLOCKS))
                for n in range(BLOCKS):
                    pe.wait_ge(*f["xh"](n + 1))
                    for c, m in enumerate(HROWS):
                        if n >= 1:
                            pe.wait_ge(*f["hid"](3 * (n - 1) + c + 1))
                        pe.matmul(bank[c][0:m, :], R[f"f0_w1{l}"][:, HID + c * P:HID + c * P + m], hT[:, blk(n)],
                                  start=True, stop=True).then_inc(f["g"].sem, 1)
                        pe.matmul(bank[3 + c][0:m, :], R[f"f0_w1{l}"][:, c * P:c * P + m], hT[:, blk(n)],
                                  start=True, stop=True).then_inc(f["a"].sem, 1)
                    if n >= 2:
                        pe.wait_ge(*f["y"](n - 1))
                    for c, m in enumerate(HROWS):
                        pe.wait_ge(*f["hid"](3 * n + c + 1))
                        mm = pe.matmul(bank[6 + n % 2], R[f"f0_w2{l}"][0:m, c, :], hid[0:m, c, :], start=(c == 0), stop=(c == HCH - 1))
                    mm.then_inc(f["down"].sem, 1)
                barrier(pe, f"f0_mlp{l}")
            barrier(pe, "gate0")
            layer_norm(LN[1])
            barrier(pe, "ln1")

            weights_in(pe, "a1")
            for n in range(BLOCKS):
                pe.matmul(bank[n][0:32, :], R["a1_wkv"], xnT[:, blk(n)], start=True, stop=True).then_inc(PREP["a1"]["ckv"].sem, 1)
            pe.wait_ge(*PREP["a1"]["ckvo"](BLOCKS))
            projections(PREP["a1"], R["a1_qk"], 4)
            barrier(pe, "a1_prep")
            attention(A1, ATT["a1"], B1, ckv, 33, R["a1_wv"])
            barrier(pe, "a1")
            post(A1, POST["a1"], B1, R["a1_wo"])
            barrier(pe, "a1_post")

            weights_in(pe, "f1")

            def similar(i):
                hp, j = divmod(i, 4)
                c = (j % 2) * PH + 2 * hp + j // 2
                for n in range(BLOCKS):
                    pe.wait_ge(*PQ["qn"](4 * i + n + 1))
                    if hp >= 1 and j == 0:
                        pe.wait_ge(*PQ["simT"](4 * (hp - 1) + n + 1))
                    mm = pe.matmul(bank[4 + n][32 * j:32 * j + 32, :], R["f1_keys"][:, c, :], qn[:, i % 2, blk(n)], start=True, stop=True)
                mm.then_inc(PQ["sim"].sem, 1)

            for i in range(16):
                hp, j = divmod(i, 4)
                c = (j % 2) * PH + 2 * hp + j // 2
                for n in range(BLOCKS):
                    if i >= 1:
                        pe.wait_ge(*PQ["qn"](4 * (i - 1) + n + 1))
                    pe.matmul(bank[n], R["f1_wq"][:, c * P:(c + 1) * P], xnT[:, blk(n)], start=True, stop=True).then_inc(PQ["q"].sem, 1)
                if i >= 1:
                    similar(i - 1)
            similar(15)
            barrier(pe, "f1_q")

            def hidden(t):
                for half in range(2):
                    i = 2 * t + half
                    if i >= 2:
                        pe.wait_ge(*PK["gd"](i - 1))
                    pe.matmul(bank[2 + half], xnT[:, t * P:(t + 1) * P], R["f1_down"][:, half * 512:(half + 1) * 512],
                              start=True, stop=True).then_inc(PK["hd"].sem, 1)

            def lists(t):
                if t >= 2:
                    pe.wait_ge(*PK["tm"](t - 1))
                for hp in range(4):
                    mm = pe.transpose(bank[t % 2][:, hp * P:(hp + 1) * P], simT[:, hp, t * P:(t + 1) * P], R["ident"][:, :])
                mm.then_inc(PK["turn"].sem, 1)

            def experts_out(t):
                pe.wait_ge(*PK["hw"](t + 1))
                for half in range(2):
                    i = 2 * t + half
                    if i >= 2:
                        pe.wait_ge(*PK["hwT"](i - 1))
                    for c in range(4):
                        k = 4 * half + c
                        mm = pe.transpose(bank[4 + half][:, c * P:(c + 1) * P], Wd[:, t % 2, k * P:(k + 1) * P], R["ident"][:, :])
                    mm.then_inc(PK["wt2"].sem, 1)
                if t >= 2:
                    pe.wait_ge(*PK["z2"](t - 1))
                for k in range(EXPCH):
                    if k % 4 == 0:
                        pe.wait_ge(*PK["hwT"](2 * t + k // 4 + 1))
                    mm = pe.matmul(bank[6 + t % 2][:, 0:P], R["f1_up"][:, k, :], hwT[:, k, :], start=(k == 0), stop=(k == EXPCH - 1))
                mm.then_inc(PK["out"].sem, 1)

            lists(0)
            hidden(0)
            for t in range(TILES):
                if t + 1 < TILES:
                    lists(t + 1)
                    hidden(t + 1)
                if t >= 1:
                    experts_out(t - 1)
            experts_out(TILES - 1)
            barrier(pe, "f1_tm")
            barrier(pe, "gate1")
            layer_norm(LN[2])
            barrier(pe, "ln2")
            pe.wait_ge(*F2["signs"](1))
            for n in range(BLOCKS):
                pe.matmul(bank[n], signs, xnT[:, blk(n)], start=True, stop=True).then_inc(F2["z"].sem, 1)
            barrier(pe, "f2")
            barrier(pe, "gate2")
            layer_norm(LN[3])
            barrier(pe, "ln3")
            weights_in(pe, "a3")
            projections(PREP["a3"], R["a3_qk"], 2)
            pe.wait_ge(*LAM["prod"](1))
            pe.wait_ge(*PREP["a3"]["raw"](8))
            pe.matmul(bank[7][:, 0:2], ones[0:4, :], small[0:4, 0:2], start=True, stop=True).then_inc(LAM["sum"].sem, 1)
            barrier(pe, "a3_prep")
            attention(A3, ATT["a3"], B3, xnT, P, R["a3_wv"])
            barrier(pe, "a3")
            post(A3, POST["a3"], B3, R["a3_wo"])
            barrier(pe, "a3_post")
            weights_in(pe, "f3")
            for t in range(TILES):
                mm = pe.matmul(bank[0][:, t * E3:(t + 1) * E3], xnT[:, t * P:(t + 1) * P], R["f3_wr"], start=True, stop=True)
            mm.then_inc(MO["logit"].sem, 1)
            pe.wait_ge(*MO["wn"](1))
            for n in range(BLOCKS):
                for t in range(4):
                    mm = pe.transpose(bank[1 + n % 2][0:E3, t * P:(t + 1) * P], r3[3][:, 4 * n + t, :], R["ident"][:, :])
                mm.then_inc(MO["turn"].sem, 1)
                pe.wait_ge(*MO["wT"](n + 1))

            def up(k):
                n, i = divmod(k, 32)
                ex, c = divmod(i, 4)
                if c == 0:
                    x = k // 4
                    if x >= 2:
                        pe.wait_ge(*MO["gw"](4 * (x - 1)))
                    pe.matmul(bank[1 + x % 2], R["f3_selw"][:, ex, :], wT3[0:E3, blk(n)], start=True, stop=True) \
                      .then_inc(MO["wb"].sem, 1)
                if k >= 3:
                    pe.wait_ge(*MO["gelu"](k - 2))
                pe.matmul(bank[3 + k % 3], R["f3_w1"][:, ex, c * P:(c + 1) * P], xnT[:, blk(n)], start=True, stop=True) \
                  .then_inc(MO["h"].sem, 1)

            def down(k):
                n, i = divmod(k, 32)
                ex, c = divmod(i, 4)
                pe.wait_ge(*MO["gw"](k + 1))
                if i == 0 and n >= 2:
                    pe.wait_ge(*MO["z"](n - 1))
                pe.matmul(bank[6 + n % 2], R["f3_w2"][:, ex, c * P:(c + 1) * P], gw3[:, k % 4, :], start=(i == 0), stop=False)
                if i == 31:
                    pe.matmul(bank[6 + n % 2], R["f3_b2"], wT3[0:E3, blk(n)], start=False, stop=True).then_inc(MO["out"].sem, 1)

            for k in range(32 * BLOCKS):
                up(k)
                if k >= 2:
                    down(k - 2)
            down(32 * BLOCKS - 2)
            down(32 * BLOCKS - 1)
            barrier(pe, "f3")
            barrier(pe, "gate3")
            for n in range(BLOCKS):
                for t in range(4):
                    tok = n * BL + t * P
                    mm = pe.transpose(bank[n][:, t * P:(t + 1) * P], xT[:, tok:tok + P], R["ident"][:, :])
                mm.then_inc(IO["back"].sem, 1)
            barrier(pe, "store")

        @block.scalar
        def _(act):
            def exp_and_log():
                act.preload_act_table_set("natural_log_exp_and_others")

            def rsqrt(e, n, src, dst):
                act.activation(dst, src, ACT.Ln, bias=eps[:, 0:1]).then_inc(e["log"].sem, 1)
                act.wait_ge(*e["log"](n + 1))
                act.activation(dst, dst, ACT.Exp, scale=-0.5).then_inc(e["rstd"].sem, 1)

            def layer_norm(e):
                for n in range(BLOCKS):
                    act.wait_ge(*e["cent"](n + 1))
                    act.activation(u2[:, blk(n)], u1[:, blk(n)], ACT.Square).then_inc(e["sq"].sem, 1)
                for n in range(BLOCKS):
                    act.wait_ge(*e["var"](n + 1))
                    rsqrt(e, n, bank[4 + n], u3[:, blk(n)])

            def split(e, PB, gelu=False):
                _, _, qk, parts = PB
                for n in range(BLOCKS):
                    for x in range(2):
                        i = 2 * n + x
                        act.wait_ge(*e["raw"](i + 1))
                        if gelu:
                            act.activation(qk[:, x, :], qk[:, x, :], ACT.Gelu).then_inc(e["gelu"].sem, 1)
                            act.wait_ge(*e["gelu"](i + 1))
                        act.activation(parts[:, x, 0, blk(n)], qk[:, x, :], ACT.Copy).then_inc(e["hi"].sem, 1)
                    for x in range(2):
                        i = 2 * n + x
                        act.wait_ge(*e["r1"](i + 1))
                        act.activation(parts[:, x, 1, blk(n)], PB[0][:, x, :], ACT.Copy).then_inc(e["mid"].sem, 1)

            def attention(a, e, B):
                def high(s):
                    r = s * a.ring + a.ring - 1
                    act.wait_ge(*e["scored"](r + 1))
                    if s >= 2 and a.split:
                        act.wait_ge(*e["rows"]((s - 1) * 16 * 2 * a.chunks))
                    act.activation(mT[0:a.heads, s % 2, :], score_ring[r % 2][0:a.heads, :], ACT.Copy, scale=-1.0) \
                       .then_inc(e["high"].sem, 1)

                def take(s, q):
                    half, qb, segs, first, last = a.b_quads[q]
                    f = s * a.fills + half * SB + qb
                    b, g = divmod(s, a.groups)
                    act.wait_ge(*e["summed"](s * a.quads + q + 1))
                    t = slice(b * SEQ + qb * BL, b * SEQ + (qb + 1) * BL)
                    act.activation(B.o[:, half, g, t], bank[a.sum_banks[f % len(a.sum_banks)]], ACT.Copy).then_inc(e["taken"].sem, 1)
                    if not a.split:
                        act.activation(B.logden[:, g, t], bank[7], ACT.Ln).then_inc(e["taken"].sem, 1)

                high(0)
                for s in range(a.steps):
                    for q in range(a.quads):
                        segs = a.b_quads[q][2]
                        cols = sum(x[2] - x[1] for x in segs)
                        quad = s * a.quads + q
                        for j in range(a.perbank):
                            n = quad * a.perbank + j
                            act.wait_ge(*e["logits"](n + 1))
                            if n >= 8:
                                act.wait_ge(*e["summed"]((n - 8) // a.perbank + 1))
                            act.activation(B.PT[:, n % 8, 0:cols], bank[a.logit_banks[n % len(a.logit_banks)]][:, 0:cols], ACT.Exp, scale=a.scale) \
                               .then_inc(e["probs"].sem, 1)
                            if n - s * a.total == min(a.sent_at[-1] + 2, a.total - 1) and s + 1 < a.steps:
                                high(s + 1)
                            if j == (2 if a.halves == 2 else a.perbank - 1) and q >= 1 and a.b_quads[q - 1][4]:
                                take(s, q - 1)
                    take(s, a.quads - 1)

            def post(a, e, B, bias=None):
                i = 0
                for n in range(BLOCKS):
                    for hg in range(a.halves * 4):
                        act.wait_ge(*e["den"](i + 1))
                        if i >= 2:
                            act.wait_ge(*e["norm"](i - 1))
                        act.activation(B.PT[:, i % 2, :], bank[i % 2], ACT.Ln).then_inc(e["log"].sem, 1)
                        act.wait_ge(*e["log"](i + 1))
                        act.activation(B.PT[:, i % 2, :], B.PT[:, i % 2, :], ACT.Exp, scale=-1.0).then_inc(e["inv"].sem, 1)
                        i += 1
                for n in range(BLOCKS):
                    if a.halves == 2:
                        for g in range(4):
                            k = 4 * n + g
                            act.wait_ge(*e["od"](k + 1))
                            act.activation(B.o[:, 1, g, blk(n)], B.o[:, 0, g, blk(n)], ACT.Square).then_inc(e["sq"].sem, 1)
                        for g in range(4):
                            k = 4 * n + g
                            act.wait_ge(*e["ms"](k + 1))
                            if k >= 4:
                                act.wait_ge(*e["on"](k - 3))
                            act.activation(B.PT[:, 4 + k % 4, :], bank[4 + k % 2], ACT.Ln, bias=eps[:, 0:1]).then_inc(e["log2"].sem, 1)
                            act.wait_ge(*e["log2"](k + 1))
                            act.activation(B.PT[:, 4 + k % 4, :], B.PT[:, 4 + k % 4, :], ACT.Exp, scale=-0.5).then_inc(e["rstd"].sem, 1)
                    act.wait_ge(*e["out"](n + 1))
                    if bias is None:
                        act.activation(sT[:, blk(n)], bank[2 + n % 2], ACT.Copy).then_inc(e["s"].sem, 1)
                    else:
                        act.activation(sT[:, blk(n)], bank[2 + n % 2], ACT.Identity, bias=bias).then_inc(e["s"].sem, 1)

            def gate(k, src):
                act.activation(u1, src[:, :], ACT.Silu).then_inc(GATE[k]["silu"].sem, 1)

            exp_and_log()
            for n in range(BLOCKS):
                act.wait_ge(*IO["turned"](n + 1))
                act.activation(xT[:, blk(n)], bank[n], ACT.Copy).then_inc(IO["x"].sem, 1)
            barrier(act, "load")
            layer_norm(LN[0])
            barrier(act, "ln0")
            split(PREP["a0"], PB0)
            barrier(act, "a0_prep")
            attention(A0, ATT["a0"], B0)
            barrier(act, "a0")
            post(A0, POST["a0"], B0)
            barrier(act, "a0_post")
            def inverse_norm(e, i):
                act.wait_ge(*e["clamp"](i + 1))
                act.activation(fd[:, i % 2, :], fd[:, i % 2, :], ACT.Ln).then_inc(e["log"].sem, 1)
                act.wait_ge(*e["log"](i + 1))
                act.activation(fd[:, i % 2, :], fd[:, i % 2, :], ACT.Exp, scale=-0.5).then_inc(e["inv"].sem, 1)

            for l in range(DEPTH):
                for b in range(BATCH):
                    e = FP[l, b]
                    for i in range(16):
                        act.wait_ge(*e["proj"](i + 1))
                        if i >= 2:
                            act.wait_ge(*e["nrm"](i - 1))
                        act.activation(fa[:, i % 2, :], bank[i % 2], ACT.Square).then_inc(e["sq"].sem, 1)
                        if i >= 1:
                            inverse_norm(e, i - 1)
                    inverse_norm(e, 15)
                    barrier(act, f"f0_prep{l}{b}")
                    attention(F0, FA[l, b], BF)
                    barrier(act, f"f0_att{l}{b}")
                    for g in range(4):
                        act.activation(BF.logden[:, g, :], BF.logden[:, g, :], ACT.Exp, scale=-1.0).then_inc(FO[l, b]["inv"].sem, 1)
                    barrier(act, f"f0_out{l}{b}")
                f = FM[l]
                for n in range(BLOCKS):
                    act.wait_ge(*LNF[l]["cent"](n + 1))
                    act.activation(BF.PT[:, 4 + n, :], BF.PT[:, n, :], ACT.Square).then_inc(LNF[l]["sq"].sem, 1)
                for n in range(BLOCKS):
                    act.wait_ge(*LNF[l]["var"](n + 1))
                    rsqrt(LNF[l], n, bank[4 + n], BF.PT[:, 4 + n, :])
                weights_in(act, f"f0{l}")
                for n in range(BLOCKS):
                    for c, m in enumerate(HROWS):
                        k = 3 * n + c
                        act.wait_ge(*f["g"](k + 1))
                        if k >= 3:
                            act.wait_ge(*f["hid"](k - 2))
                        act.activation(gel[0:m, c, :], bank[c][0:m, :], ACT.Gelu, bias=R[f"f0_b1{l}"][0:m, 3 + c:4 + c]) \
                           .then_inc(f["gelu"].sem, 1)
                exp_and_log()
                barrier(act, f"f0_mlp{l}")
            gate(0, xnT)
            exp_and_log()
            barrier(act, "gate0")
            layer_norm(LN[1])
            barrier(act, "ln1")
            weights_in(act, "a1")
            for n in range(BLOCKS):
                act.wait_ge(*PREP["a1"]["ckv"](n + 1))
                act.activation(ckv[0:32, blk(n)], bank[n][0:32, :], ACT.Gelu, bias=R["a1_bkv"]).then_inc(PREP["a1"]["ckvo"].sem, 1)
            split(PREP["a1"], PB1, gelu=True)
            exp_and_log()
            barrier(act, "a1_prep")
            attention(A1, ATT["a1"], B1)
            barrier(act, "a1")
            post(A1, POST["a1"], B1, bias=R["a1_b"][:, 4:5])
            barrier(act, "a1_post")
            for i in range(16):
                hp, j = divmod(i, 4)
                act.wait_ge(*PQ["mv"](i + 1))
                act.activation(bnx[:, 0, i:i + 1], bnmv[:, i, 1:2], ACT.Ln, bias=eps[:, 0:1]).then_inc(PQ["log"].sem, 1)
                act.wait_ge(*PQ["log"](i + 1))
                act.activation(bnx[:, 1, i:i + 1], bnx[:, 0, i:i + 1], ACT.Exp, scale=-0.5).then_inc(PQ["rstd"].sem, 1)
                act.wait_ge(*PQ["sh"](i + 1))
                if i >= 2:
                    act.wait_ge(*PQ["sim"](i - 1))
                for n in range(BLOCKS):
                    act.activation(qn[:, i % 2, blk(n)], bank[n], ACT.Identity, scale=bnx[:, 2, i:i + 1], bias=bnx[:, 3, i:i + 1]) \
                       .then_inc(PQ["qn"].sem, 1)
                if j == 0 and hp >= 1:
                    for n in range(BLOCKS):
                        act.wait_ge(*PQ["sim"](4 * hp))
                        act.activation(simT[:, hp - 1, blk(n)], bank[4 + n], ACT.Copy).then_inc(PQ["simT"].sem, 1)
            for n in range(BLOCKS):
                act.wait_ge(*PQ["sim"](16))
                act.activation(simT[:, 3, blk(n)], bank[4 + n], ACT.Copy).then_inc(PQ["simT"].sem, 1)
            barrier(act, "f1_q")

            def experts_out(t):
                for half in range(2):
                    i = 2 * t + half
                    act.wait_ge(*PK["wt2"](i + 1))
                    if t >= 1:
                        act.wait_ge(*PK["out"](t))
                    act.activation(hwT[:, 4 * half:4 * half + 4, :], bank[4 + half].rearrange("p (c t) -> p c t", c=4), ACT.Copy) \
                       .then_inc(PK["hwT"].sem, 1)
                act.wait_ge(*PK["out"](t + 1))
                act.activation(zT[:, t * P:(t + 1) * P], bank[6 + t % 2][:, 0:P], ACT.Copy).then_inc(PK["z2"].sem, 1)

            def lists(t):
                act.wait_ge(*PK["turn"](t + 1))
                if t >= 2:
                    act.wait_ge(*PK["sub"](2 * t - 2))
                act.activation(sim[:, t % 2], bank[t % 2].rearrange("p (h x k) -> p h x k", h=PH, x=2), ACT.Copy).then_inc(PK["tm"].sem, 1)

            lists(0)
            for t in range(TILES):
                for half in range(2):
                    act.wait_ge(*PK["hd"](2 * t + half + 1))
                    if t >= 2:
                        act.wait_ge(*PK["hw"](t - 1))
                    act.activation(gd[:, t % 2, half * 512:(half + 1) * 512], bank[2 + half], ACT.Gelu_apprx_tanh).then_inc(PK["gd"].sem, 1)
                act.wait_ge(*PK["sub8"](t + 1))
                act.activation(es8, es8, ACT.Exp).then_inc(PK["e8"].sem, 1)
                for x in range(2):
                    act.wait_ge(*PK["sub"](2 * t + x + 1))
                    act.activation(exy[:, t % 2, x], exy[:, t % 2, x], ACT.Exp).then_inc(PK["exy"].sem, 1)
                if t + 1 < TILES:
                    lists(t + 1)
                act.wait_ge(*PK["rank"](2 * t + 1))
                for h in range(PH):
                    i = PH * t + h
                    if i >= 2:
                        act.wait_ge(*PK["m"](i - 1))
                    act.activation(rows_of[:, i % 2].rearrange("p (a b) -> p a b", a=NK),
                                   rank[:, 0, h, :].unsqueeze(2).broadcast_to((P, NK, NK)), ACT.Copy).then_inc(PK["spread"].sem, 1)
                if t >= 1:
                    experts_out(t - 1)
            experts_out(TILES - 1)
            barrier(act, "f1_tm")
            gate(1, zT)
            exp_and_log()
            barrier(act, "gate1")
            layer_norm(LN[2])
            barrier(act, "ln2")
            weights_in(act, "f2")
            act.activation(signs, R["f2_w"], ACT.Sign).then_inc(F2["signs"].sem, 1)
            for n in range(BLOCKS):
                act.wait_ge(*F2["z"](n + 1))
                act.activation(zT[:, blk(n)], bank[n], ACT.Copy).then_inc(F2["out"].sem, 1)
            barrier(act, "f2")
            gate(2, zT)
            exp_and_log()
            barrier(act, "gate2")
            layer_norm(LN[3])
            barrier(act, "ln3")
            split(PREP["a3"], PB3)
            act.wait_ge(*LAM["sum"](1))
            act.activation(small[:, 4:6], bank[7][:, 0:2], ACT.Exp).then_inc(LAM["exp"].sem, 1)
            barrier(act, "a3_prep")
            attention(A3, ATT["a3"], B3)
            barrier(act, "a3")
            post(A3, POST["a3"], B3, bias=R["a3_vec"][:, 1:2])
            barrier(act, "a3_post")
            act.wait_ge(*MO["sub"](1))
            act.activation(r3[1], r3[0], ACT.Exp).then_inc(MO["exp"].sem, 1)
            for n in range(BLOCKS):
                act.wait_ge(*MO["turn"](n + 1))
                act.activation(wT3[0:E3, blk(n)], bank[1 + n % 2][0:E3, :], ACT.Copy).then_inc(MO["wT"].sem, 1)
            weights_in(act, "f3")

            def result(n):
                act.wait_ge(*MO["out"](n + 1))
                act.activation(zT[:, blk(n)], bank[6 + n % 2], ACT.Copy).then_inc(MO["z"].sem, 1)

            for k in range(32 * BLOCKS):
                n, i = divmod(k, 32)
                act.wait_ge(*MO["h"](k + 1))
                if k >= 4:
                    act.wait_ge(*MO["gw"](k - 3))
                act.activation(g3[:, k % 4, :], bank[3 + k % 3], ACT.Gelu, bias=R["f3_b1"][:, i:i + 1]).then_inc(MO["gelu"].sem, 1)
                if i == 8 and n >= 1:
                    result(n - 1)
            result(BLOCKS - 1)
            barrier(act, "f3")
            gate(3, zT)
            barrier(act, "gate3")
            for n in range(BLOCKS):
                act.wait_ge(*IO["back"](n + 1))
                act.activation(u1[:, blk(n)], bank[n], ACT.Copy).then_inc(IO["out"].sem, 1)
            barrier(act, "store")

        @block.vector
        def _(dve):
            def layer_norm(e):
                for n in range(BLOCKS):
                    dve.wait_ge(*e["mean"](n + 1))
                    dve.tensor_tensor(u1[:, blk(n)], xT[:, blk(n)], bank[n], ALU.subtract).then_inc(e["cent"].sem, 1)
                for n in range(BLOCKS):
                    dve.wait_ge(*e["rstd"](n + 1))
                    dve.tensor_tensor(xnT[:, blk(n)], u1[:, blk(n)], u3[:, blk(n)], ALU.mult).then_inc(e["out"].sem, 1)

            def split(e, PB, rotate):
                tA, tB, qk, parts = PB
                for n in range(BLOCKS):
                    for x in range(2):
                        i = 2 * n + x
                        dve.wait_ge(*e["proj"](i + 1))
                        if n >= 1:
                            dve.wait_ge(*e["lo"](i - 1))
                        rotate(e, n, x, i, tA[:, x, :], tB[:, x, :], qk[:, x, :])
                    for x in range(2):
                        i = 2 * n + x
                        dve.wait_ge(*e["hi"](i + 1))
                        dve.tensor_tensor(tA[:, x, :], qk[:, x, :], parts[:, x, 0, blk(n)], ALU.subtract).then_inc(e["r1"].sem, 1)
                    for x in range(2):
                        i = 2 * n + x
                        dve.wait_ge(*e["mid"](i + 1))
                        dve.tensor_tensor(parts[:, x, 2, blk(n)], tA[:, x, :], parts[:, x, 1, blk(n)], ALU.subtract).then_inc(e["lo"].sem, 1)

            def attention(a, e, B):
                for s in range(a.steps):
                    for k in range(a.ring):
                        r = s * a.ring + k
                        src = score_ring[r % 2]
                        dve.wait_ge(*e["scored"](r + 1))
                        if k == 0:
                            if s >= SLOTS:
                                dve.wait_ge(*e["summed"]((s - SLOTS + 1) * a.quads))
                            if a.split:
                                if s == 0:
                                    dve.wait_ge(*e["zeroed"](1))
                                g = s % a.groups
                                dve.tensor_copy(B.V[:, s % SLOTS].rearrange("p t (j n) -> p t j n", j=4)[:, :, :, 0:8],
                                                src.rearrange("p (t n) -> p t n", t=QT)[:, :, 32 * g:32 * g + 32]
                                                .rearrange("p t (j e) -> p t j e", j=4)).then_inc(e["maxed"].sem, 1)
                            else:
                                dve.tensor_copy(B.V[:, s % SLOTS], src.rearrange("p (t n) -> p t n", t=QT)).then_inc(e["maxed"].sem, 1)
                        elif k == a.ring - 1:
                            dve.wait_ge(*e["high"](s + 1))
                            dve.scalar_tensor_tensor(out=mT[32:32 + a.heads, s % 2, :], in0=src[0:a.heads, :], scalar=-1.0,
                                                     in1=mT[0:a.heads, s % 2, :], op0=ALU.mult, op1=ALU.subtract) \
                               .then_inc(e["maxed"].sem, 1)
                        else:
                            qt, h0, n, wide, k0, k1 = a.a_units[k - 1]
                            if k == 1 and s >= 2:
                                dve.wait_ge(*e["scored"]((s - 1) * a.ring))
                            dve.tensor_reduce(m_tm[:, s % 2, qt, h0:h0 + n],
                                              src[:, 0:n * wide].rearrange("p (h k) -> p h k", h=n)[:, :, 0:k1 - k0],
                                              AX_X, ALU.max).then_inc(e["maxed"].sem, 1)

            def post(a, e, B, vec=None):
                i = 0
                for n in range(BLOCKS):
                    for hg in range(a.halves * 4):
                        h, g = divmod(hg, 4)
                        dve.wait_ge(*e["inv"](i + 1))
                        dve.tensor_tensor(B.o[:, h, g, blk(n)], B.o[:, h, g, blk(n)], B.PT[:, i % 2, :], ALU.mult).then_inc(e["norm"].sem, 1)
                        i += 1
                if a.halves == 2:
                    for n in range(BLOCKS):
                        for g in range(4):
                            k = 4 * n + g
                            dve.wait_ge(*e["norm"](8 * n + 4 + g + 1))
                            dve.scalar_tensor_tensor(out=B.o[:, 0, g, blk(n)], in0=B.o[:, 1, g, blk(n)], scalar=small[:, 7:8],
                                                     in1=B.o[:, 0, g, blk(n)], op0=ALU.mult, op1=ALU.add).then_inc(e["od"].sem, 1)
                        for g in range(4):
                            k = 4 * n + g
                            dve.wait_ge(*e["rstd"](k + 1))
                            dve.scalar_tensor_tensor(out=B.o[:, 0, g, blk(n)], in0=B.o[:, 0, g, blk(n)], scalar=vec,
                                                     in1=B.PT[:, 4 + k % 4, :], op0=ALU.mult, op1=ALU.mult).then_inc(e["on"].sem, 1)

            def gate(k, s):
                dve.wait_ge(*GATE[k]["silu"](1))
                dve.tensor_tensor(u2, u1, s[:, :], ALU.mult).then_inc(GATE[k]["mix"].sem, 1)
                dve.wait_ge(*GATE[k]["mix"](1))
                dve.tensor_tensor(xT[:, :], xT[:, :], u2, ALU.add).then_inc(GATE[k]["x"].sem, 1)

            def shift(e, src):
                s = src[:, :].rearrange("p (b t) -> p b t", b=BATCH)
                h = hT[:, :].rearrange("p (b t) -> p b t", b=BATCH)
                dve.tensor_copy(hT[0:64, :], src[0:64, :]).then_inc(e["h"].sem, 1)
                dve.tensor_copy(h[64:P, :, 1:SEQ], s[64:P, :, 0:SEQ - 1]).then_inc(e["h"].sem, 1)
                dve.memset(h[64:P, :, 0:1], 0.0).then_inc(e["h"].sem, 1)

            dve.memset(ones[:, :], 1.0)
            dve.memset(mean_of[:, :], 1.0 / D)
            dve.memset(eps[:, :], EPS)
            dve.memset(mT[:, :, :], 0.0)
            dve.memset(m_tm[:, :, :, :], 0.0)
            barrier(dve, "load")
            layer_norm(LN[0])
            barrier(dve, "ln0")
            weights_in(dve, "a0")

            def rotate0(e, n, x, i, A, Bt, q):
                dve.tensor_tensor(A, bank[(n % 2) * 4 + 2 * x], R["a0_cos"][:, (n % SB) * BL:(n % SB + 1) * BL], ALU.mult).then_inc(e["rc"].sem, 1)
                dve.tensor_tensor(Bt, bank[(n % 2) * 4 + 2 * x + 1], R["a0_sin"][:, (n % SB) * BL:(n % SB + 1) * BL], ALU.mult).then_inc(e["rs"].sem, 1)
                dve.wait_ge(*e["rc"](i + 1))
                dve.wait_ge(*e["rs"](i + 1))
                dve.tensor_tensor(q, A, Bt, ALU.add).then_inc(e["raw"].sem, 1)

            split(PREP["a0"], PB0, rotate0)
            barrier(dve, "a0_prep")
            attention(A0, ATT["a0"], B0)
            barrier(dve, "a0")
            post(A0, POST["a0"], B0)
            barrier(dve, "a0_post")
            def outs(k):
                return k if k <= 8 else 8 + 2 * (k - 8)

            def scale_out(e, i):
                x, c, n = i // 8, i // 2 % 4, i % 2
                dve.wait_ge(*e["sum"](i + 1))
                dve.wait_ge(*e["inv"](i + 1))
                if x == 0:
                    dve.tensor_tensor(BF.qall[:, c, 0, blk(n)], fb[:, i % 2, :], fd[:, i % 2, :], ALU.mult).then_inc(e["out"].sem, 1)
                else:
                    for h in range(2):
                        r = slice(64 * h, 64 * h + 64)
                        dve.tensor_tensor(BF.kall[r, c, 0, h, blk(n)], fb[r, i % 2, :], fd[r, i % 2, :], ALU.mult).then_inc(e["out"].sem, 1)

            for l in range(DEPTH):
                V = R[f"f0_vec{l}"]
                shift(FS[l], xnT)
                for b in range(BATCH):
                    e = FP[l, b]
                    weights_in(dve, f"f0{l}")
                    for i in range(16):
                        x, c, n = i // 8, i // 2 % 4, i % 2
                        tab = R["f0_tab"][:, 2 * x:2 * x + 2, n * BL:(n + 1) * BL]
                        dve.wait_ge(*e["proj"](i + 1))
                        dve.wait_ge(*e["sq"](i + 1))
                        if i >= 2:
                            dve.wait_ge(*e["out"](outs(i - 1)))
                        dve.scalar_tensor_tensor(out=fb[:, i % 2, :], in0=bank[i % 2], scalar=V[:, 2 * x:2 * x + 1],
                                                 in1=tab[:, 0, :], op0=ALU.mult, op1=ALU.mult).then_inc(e["qc"].sem, 1)
                        dve.wait_ge(*e["rot"](i + 1))
                        dve.scalar_tensor_tensor(out=fc[:, i % 2, :], in0=bank[2 + i % 2], scalar=V[:, 2 * x + 1:2 * x + 2],
                                                 in1=tab[:, 1, :], op0=ALU.mult, op1=ALU.mult).then_inc(e["qr"].sem, 1)
                        if i >= 1:
                            scale_out(e, i - 1)
                        dve.wait_ge(*e["nrm"](i + 1))
                        if i >= 2:
                            dve.wait_ge(*e["out"](outs(i - 1)))
                        dve.tensor_scalar(fd[:, i % 2, :], bank[4 + i % 2], 1e-24, None, ALU.max).then_inc(e["clamp"].sem, 1)
                    scale_out(e, 15)
                    barrier(dve, f"f0_prep{l}{b}")
                    attention(F0, FA[l, b], BF)
                    barrier(dve, f"f0_att{l}{b}")
                    f = FO[l, b]
                    for g in range(4):
                        dve.wait_ge(*f["inv"](g + 1))
                        dve.tensor_tensor(BF.o[:, 0, g, :], BF.o[:, 0, g, :], BF.logden[:, g, :], ALU.mult).then_inc(f["norm"].sem, 1)
                    for n in range(SB):
                        s = slice(b * SEQ + n * BL, b * SEQ + (n + 1) * BL)
                        dve.wait_ge(*f["o"](n + 1))
                        dve.tensor_tensor(xnT[:, s], bank[n], xnT[:, s], ALU.add).then_inc(f["y"].sem, 1)
                    barrier(dve, f"f0_out{l}{b}")
                f = FM[l]
                shift(FMS[l], xnT)
                for n in range(BLOCKS):
                    dve.wait_ge(*LNF[l]["mean"](n + 1))
                    dve.tensor_tensor(BF.PT[:, n, :], hT[:, blk(n)], bank[n], ALU.subtract).then_inc(LNF[l]["cent"].sem, 1)
                for n in range(BLOCKS):
                    dve.wait_ge(*LNF[l]["rstd"](n + 1))
                    dve.tensor_tensor(BF.PT[:, n, :], BF.PT[:, n, :], BF.PT[:, 4 + n, :], ALU.mult).then_inc(f["norm"].sem, 1)
                    dve.wait_ge(*f["norm"](n + 1))
                    dve.tensor_scalar(hT[:, blk(n)], BF.PT[:, n, :], V[:, 4:5], V[:, 5:6], ALU.mult, ALU.add).then_inc(f["xh"].sem, 1)

                def residual(n):
                    dve.wait_ge(*f["down"](n + 1))
                    dve.scalar_tensor_tensor(out=xnT[:, blk(n)], in0=bank[6 + n % 2], scalar=V[:, 6:7], in1=xnT[:, blk(n)],
                                             op0=ALU.add, op1=ALU.add).then_inc(f["y"].sem, 1)

                for n in range(BLOCKS):
                    for c, m in enumerate(HROWS):
                        k = 3 * n + c
                        dve.wait_ge(*f["a"](k + 1))
                        dve.wait_ge(*f["gelu"](k + 1))
                        if n >= 1:
                            dve.wait_ge(*f["down"](n))
                        dve.scalar_tensor_tensor(out=hid[0:m, c, :], in0=bank[3 + c][0:m, :], scalar=R[f"f0_b1{l}"][0:m, c:c + 1],
                                                 in1=gel[0:m, c, :], op0=ALU.add, op1=ALU.mult).then_inc(f["hid"].sem, 1)
                    residual(n)
                barrier(dve, f"f0_mlp{l}")
            gate(0, sT)
            barrier(dve, "gate0")
            layer_norm(LN[1])
            barrier(dve, "ln1")
            weights_in(dve, "a1")
            dve.memset(ckv[32:33, :], 1.0)

            def rotate1(e, n, x, i, A, Bt, q):
                t = slice((n % SB) * BL, (n % SB + 1) * BL)
                dve.scalar_tensor_tensor(out=A, in0=bank[(n % 2) * 4 + 2 * x], scalar=R["a1_b"][:, 2 * x:2 * x + 1],
                                         in1=R["a1_cos"][:, t], op0=ALU.add, op1=ALU.mult).then_inc(e["rc"].sem, 1)
                dve.scalar_tensor_tensor(out=Bt, in0=bank[(n % 2) * 4 + 2 * x + 1], scalar=R["a1_b"][:, 2 * x + 1:2 * x + 2],
                                         in1=R["a1_sin"][:, t], op0=ALU.add, op1=ALU.mult).then_inc(e["rs"].sem, 1)
                dve.wait_ge(*e["rc"](i + 1))
                dve.wait_ge(*e["rs"](i + 1))
                dve.tensor_tensor(q, A, Bt, ALU.add).then_inc(e["raw"].sem, 1)

            split(PREP["a1"], PB1, rotate1)
            barrier(dve, "a1_prep")
            attention(A1, ATT["a1"], B1)
            barrier(dve, "a1")
            post(A1, POST["a1"], B1)
            barrier(dve, "a1_post")
            weights_in(dve, "f1")
            for i in range(16):
                hp, j = divmod(i, 4)
                c = (j % 2) * PH + 2 * hp + j // 2
                for n in range(BLOCKS):
                    dve.wait_ge(*PQ["q"](4 * i + n + 1))
                    dve.bn_stats(bnst[:, i, 6 * n:6 * n + 6], bank[n]).then_inc(PQ["st"].sem, 1)
                dve.wait_ge(*PQ["st"](4 * i + 4))
                dve.bn_aggr(bnmv[:, i, :], bnst[:, i, :]).then_inc(PQ["mv"].sem, 1)
                dve.wait_ge(*PQ["rstd"](i + 1))
                dve.tensor_tensor(bnx[:, 2, i:i + 1], bnx[:, 1, i:i + 1], R["f1_gb"][:, 0, c:c + 1], ALU.mult).then_inc(PQ["sc"].sem, 1)
                dve.wait_ge(*PQ["sc"](i + 1))
                dve.tensor_tensor(bnx[:, 0, i:i + 1], bnmv[:, i, 0:1], bnx[:, 2, i:i + 1], ALU.mult).then_inc(PQ["tmp"].sem, 1)
                dve.wait_ge(*PQ["tmp"](i + 1))
                dve.tensor_tensor(bnx[:, 3, i:i + 1], R["f1_gb"][:, 1, c:c + 1], bnx[:, 0, i:i + 1], ALU.subtract).then_inc(PQ["sh"].sem, 1)
            barrier(dve, "f1_q")
            def weighted(t):
                dve.wait_ge(*PK["acc"](PH * (t + 1)))
                dve.wait_ge(*PK["gd"](2 * t + 2))
                dve.tensor_tensor(Wd[:, t % 2], Wd[:, t % 2], gd[:, t % 2], ALU.mult).then_inc(PK["hw"].sem, 1)

            for t in range(TILES):
                L = sim[:, t % 2]
                X = exy[:, t % 2]
                dve.wait_ge(*PK["tm"](t + 1))
                for i in range(16):
                    dve.max(top[:, i // 2, i % 2, :], L[:, i // 2, i % 2, :]).then_inc(PK["top"].sem, 1)
                for i in range(16):
                    dve.wait_ge(*PK["top"](16 * t + i + 1))
                    dve.max_index(idx[:, i // 2, i % 2, :], top[:, i // 2, i % 2, :], L[:, i // 2, i % 2, :]).then_inc(PK["idx"].sem, 1)
                dve.tensor_tensor(comb.rearrange("p h (a b) -> p h a b", a=TOPK),
                                  top[:, :, 0, :].unsqueeze(3).broadcast_to((P, PH, TOPK, TOPK)),
                                  top[:, :, 1, :].unsqueeze(2).broadcast_to((P, PH, TOPK, TOPK)), ALU.add).then_inc(PK["comb"].sem, 1)
                dve.wait_ge(*PK["idx"](16 * t + 16))
                for x in range(2):
                    dve.tensor_copy(idxf[:, x, :].rearrange("p (h a) -> p h a", h=PH), idx[:, :, x, :]).then_inc(PK["idxf"].sem, 1)
                dve.wait_ge(*PK["comb"](t + 1))
                for i in range(PH):
                    dve.max(sc8[:, i, :], comb[:, i, :]).then_inc(PK["sc8"].sem, 1)
                for i in range(PH):
                    dve.wait_ge(*PK["sc8"](PH * t + i + 1))
                    dve.match_replace(rep[:, i, :], sc8[:, i, :], comb[:, i, :], GONE).then_inc(PK["rep"].sem, 1)
                dve.tensor_tensor(es8, sc8, sc8[:, :, 0:1].broadcast_to((P, PH, TOPK)), ALU.subtract).then_inc(PK["sub8"].sem, 1)
                if t >= 2:
                    dve.wait_ge(*PK["acc"](PH * (t - 1)))
                for x in range(2):
                    dve.tensor_tensor(X[:, x], L[:, :, x, :], top[:, :, x, 0:1].broadcast_to((P, PH, NK)), ALU.subtract).then_inc(PK["sub"].sem, 1)
                dve.wait_ge(*PK["rep"](PH * t + PH))
                dve.tensor_scalar(comb, rep, GONE, None, ALU.is_le).then_inc(PK["mask"].sem, 1)
                dve.wait_ge(*PK["mask"](t + 1))
                dve.tensor_reduce(nsel.rearrange("p (h a) -> p h a", h=PH), comb.rearrange("p h (a b) -> p h a b", a=TOPK),
                                  AX_X, ALU.add).then_inc(PK["nsel"].sem, 1)
                dve.wait_ge(*PK["e8"](t + 1))
                dve.tensor_reduce(zr[:, 0, :], es8, AX_X, ALU.add).then_inc(PK["z"].sem, 1)
                dve.wait_ge(*PK["z"](t + 1))
                dve.reciprocal(zr[:, 1, :], zr[:, 0, :]).then_inc(PK["rz"].sem, 1)
                dve.wait_ge(*PK["exy"](2 * t + 2))
                dve.wait_ge(*PK["rz"](t + 1))
                dve.tensor_tensor(X[:, 0], X[:, 0], zr[:, 1, :].unsqueeze(2).broadcast_to((P, PH, NK)), ALU.mult).then_inc(PK["exz"].sem, 1)
                dve.wait_ge(*PK["nsel"](t + 1))
                dve.tensor_copy(nselb, nsel).then_inc(PK["nselb"].sem, 1)
                dve.wait_ge(*PK["nselb"](t + 1))
                dve.wait_ge(*PK["idxf"](2 * t + 2))
                for x in range(2):
                    i = 2 * t + x
                    if i >= 1:
                        dve.wait_ge(*PK["rank"](i))
                    full = (P, PH, NK, TOPK)
                    dve.tensor_tensor(onehot, R["iota_ka"].rearrange("p (k a) -> p k a", k=NK).unsqueeze(1).broadcast_to(full),
                                      idxf[:, x, :].rearrange("p (h a) -> p h a", h=PH).unsqueeze(2).broadcast_to(full),
                                      ALU.is_equal).then_inc(PK["eq"].sem, 1)
                    weight = nselb if x == 0 else R["rankw"][:, :]
                    dve.wait_ge(*PK["eq"](i + 1))
                    dve.tensor_tensor(onehot, onehot, weight.rearrange("p (h a) -> p h a", h=PH).unsqueeze(2).broadcast_to(full),
                                      ALU.mult).then_inc(PK["wt"].sem, 1)
                    dve.wait_ge(*PK["wt"](i + 1))
                    if x == 0 and t >= 1:
                        dve.wait_ge(*PK["spread"](PH * t))
                    dve.tensor_reduce(rank[:, x], onehot, AX_X, ALU.add).then_inc(PK["rank"].sem, 1)
                dve.wait_ge(*PK["rank"](2 * t + 2))
                dve.tensor_scalar(below, rank[:, 1], -1.0, float(TOPK), ALU.mult, ALU.add).then_inc(PK["below"].sem, 1)
                dve.wait_ge(*PK["below"](t + 1))
                for h in range(PH):
                    i = PH * t + h
                    if i >= 2:
                        dve.wait_ge(*PK["me"](i - 1))
                    dve.wait_ge(*PK["spread"](i + 1))
                    dve.tensor_tensor(pairs[:, i % 2].rearrange("p (a b) -> p a b", a=NK),
                                      rows_of[:, i % 2].rearrange("p (a b) -> p a b", a=NK),
                                      below[:, h, :].unsqueeze(1).broadcast_to((P, NK, NK)), ALU.is_gt).then_inc(PK["m"].sem, 1)
                    dve.wait_ge(*PK["m"](i + 1))
                    if i >= 8:
                        dve.wait_ge(*PK["acc"](i - 7))
                    dve.tensor_tensor(dm[:, i % 8].rearrange("p (a b) -> p a b", a=NK),
                                      pairs[:, i % 2].rearrange("p (a b) -> p a b", a=NK),
                                      X[:, 1, h, :].unsqueeze(1).broadcast_to((P, NK, NK)), ALU.mult).then_inc(PK["me"].sem, 1)
                if t >= 1:
                    weighted(t - 1)
            weighted(TILES - 1)
            barrier(dve, "f1_tm")
            gate(1, sT)
            barrier(dve, "gate1")
            layer_norm(LN[2])
            barrier(dve, "ln2")
            barrier(dve, "f2")
            gate(2, xnT)
            barrier(dve, "gate2")
            layer_norm(LN[3])
            barrier(dve, "ln3")
            weights_in(dve, "a3")
            dve.tensor_tensor(small[0:4, 0:2], R["a3_lam"][:, 0:2], R["a3_lam"][:, 2:4], ALU.mult).then_inc(LAM["prod"].sem, 1)
            dve.tensor_scalar(small[:, 8:9], R["a3_vec"][:, 0:1], 1.0 - LAMBDA_INIT, None, ALU.mult).then_inc(LAM["weight"].sem, 1)

            def rotate3(e, n, x, i, A, Bt, q):
                dve.tensor_copy(q, bank[(n % 2) * 4 + 2 * x]).then_inc(e["raw"].sem, 1)

            split(PREP["a3"], PB3, rotate3)
            dve.wait_ge(*LAM["exp"](1))
            dve.tensor_scalar(small[:, 6:7], small[:, 5:6], -LAMBDA_INIT, None, ALU.add).then_inc(LAM["part"].sem, 1)
            dve.wait_ge(*LAM["part"](1))
            dve.tensor_tensor(small[:, 7:8], small[:, 6:7], small[:, 4:5], ALU.subtract).then_inc(LAM["neg"].sem, 1)
            barrier(dve, "a3_prep")
            attention(A3, ATT["a3"], B3)
            barrier(dve, "a3")
            post(A3, POST["a3"], B3, vec=small[:, 8:9])
            barrier(dve, "a3_post")
            lg, ex, pr, wn, tops, tif, o0, o1, ti = r3
            tidx = ti.bitcast(U32)
            vmax, vsum, vinv, vden, vrd = v3
            wide = (P, TILES, E3)
            dve.wait_ge(*MO["logit"](1))
            plg = bank[0][:, 0:TILES * E3].rearrange("p (t e) -> p t e", t=TILES)
            dve.tensor_reduce(vmax, plg, AX_X, ALU.max).then_inc(MO["max"].sem, 1)
            dve.wait_ge(*MO["max"](1))
            dve.tensor_tensor(lg, plg, vmax.unsqueeze(2).broadcast_to(wide), ALU.subtract).then_inc(MO["sub"].sem, 1)
            dve.wait_ge(*MO["exp"](1))
            dve.tensor_reduce(vsum, ex, AX_X, ALU.add).then_inc(MO["sum"].sem, 1)
            dve.wait_ge(*MO["sum"](1))
            dve.reciprocal(vinv, vsum).then_inc(MO["inv"].sem, 1)
            dve.wait_ge(*MO["inv"](1))
            dve.tensor_tensor(pr, ex, vinv.unsqueeze(2).broadcast_to(wide), ALU.mult).then_inc(MO["prob"].sem, 1)
            dve.wait_ge(*MO["prob"](1))
            for t in range(TILES):
                dve.max(tops[:, t, :], pr[:, t, :]).then_inc(MO["top"].sem, 1)
            for t in range(TILES):
                dve.wait_ge(*MO["top"](t + 1))
                dve.max_index(tidx[:, t, :], tops[:, t, :], pr[:, t, :]).then_inc(MO["idx"].sem, 1)
            dve.wait_ge(*MO["idx"](TILES))
            dve.tensor_copy(tif, tidx).then_inc(MO["idxf"].sem, 1)
            dve.tensor_tensor(vden, tops[:, :, 0], tops[:, :, 1], ALU.add).then_inc(MO["den"].sem, 1)
            dve.wait_ge(*MO["idxf"](1))
            iota = R["iota"][:, 0:E3].unsqueeze(1).broadcast_to(wide)
            dve.tensor_tensor(o0, iota, tif[:, :, 0:1].broadcast_to(wide), ALU.is_equal).then_inc(MO["o0"].sem, 1)
            dve.tensor_tensor(o1, iota, tif[:, :, 1:2].broadcast_to(wide), ALU.is_equal).then_inc(MO["o1"].sem, 1)
            dve.wait_ge(*MO["den"](1))
            dve.reciprocal(vrd, vden).then_inc(MO["rden"].sem, 1)
            dve.wait_ge(*MO["o0"](1))
            dve.tensor_tensor(o0, o0, tops[:, :, 0:1].broadcast_to(wide), ALU.mult).then_inc(MO["m0"].sem, 1)
            dve.wait_ge(*MO["o1"](1))
            dve.tensor_tensor(o1, o1, tops[:, :, 1:2].broadcast_to(wide), ALU.mult).then_inc(MO["m1"].sem, 1)
            dve.wait_ge(*MO["m0"](1))
            dve.wait_ge(*MO["m1"](1))
            dve.tensor_tensor(o0, o0, o1, ALU.add).then_inc(MO["w"].sem, 1)
            dve.wait_ge(*MO["w"](1))
            dve.wait_ge(*MO["rden"](1))
            dve.tensor_tensor(wn, o0, vrd.unsqueeze(2).broadcast_to(wide), ALU.mult).then_inc(MO["wn"].sem, 1)
            for k in range(32 * BLOCKS):
                dve.wait_ge(*MO["wb"](k // 4 + 1))
                dve.wait_ge(*MO["gelu"](k + 1))
                dve.tensor_tensor(gw3[:, k % 4, :], bank[1 + k // 4 % 2], g3[:, k % 4, :], ALU.mult).then_inc(MO["gw"].sem, 1)
            barrier(dve, "f3")
            gate(3, sT)
            barrier(dve, "gate3")
            barrier(dve, "store")

        @block.gpsimd
        def _(pool):
            def rings(a, e, B, prep):
                after(pool, before(prep))
                pool.memset(B.kall.rearrange("p s c a t -> p (s c a t)").bitcast(F32), 0.0)
                pool.memset(B.qall.rearrange("p s c t -> p (s c t)").bitcast(F32), 0.0)
                pool.memset(B.V, 0.0).then_inc(POOLED.sem, 1)
                POOLED.n += 1
                pool.wait_ge(*POOLED(POOLED.n))
                pool.memset(B.V.rearrange("p s t (j n) -> p (s t j) n", j=4)[:, :, 8:9], 1.0).then_inc(e["zeroed"].sem, 1)

            rings(A0, ATT["a0"], B0, "a0_prep")
            for l in range(DEPTH):
                for b in range(BATCH):
                    e = FP[l, b]
                    if (l, b) == (0, 0):
                        after(pool, "a0_post")
                        pool.memset(BF.kall, 0.0).then_inc(FA[l, b]["zeroed"].sem, 1)
                        pool.wait_ge(*FA[l, b]["zeroed"](1))
                    for i in range(16):
                        pool.wait_ge(*e["qc"](i + 1))
                        pool.wait_ge(*e["qr"](i + 1))
                        pool.tensor_tensor(fb[:, i % 2, :], fb[:, i % 2, :], fc[:, i % 2, :], ALU.add).then_inc(e["sum"].sem, 1)
            rings(A1, ATT["a1"], B1, "a1_prep")
            for t in range(TILES):
                for h in range(PH):
                    i = PH * t + h
                    pool.wait_ge(*PK["me"](i + 1))
                    src = dm[:, i % 8].rearrange("p (a b) -> p a b", a=NK)
                    ex = exy[:, t % 2, 0, h, :].unsqueeze(2).broadcast_to((P, NK, NK))
                    W = Wd[:, t % 2].rearrange("p (a b) -> p a b", a=NK)
                    if h == 0:
                        if t >= 2:
                            pool.wait_ge(*PK["wt2"](2 * (t - 1)))
                        pool.tensor_tensor(W, src, ex, ALU.mult).then_inc(PK["acc"].sem, 1)
                    else:
                        pool.tensor_tensor(src, src, ex, ALU.mult).then_inc(PK["w"].sem, 1)
                        pool.wait_ge(*PK["w"](i - t))
                        pool.wait_ge(*PK["acc"](i))
                        pool.tensor_tensor(W, W, src, ALU.add).then_inc(PK["acc"].sem, 1)
            rings(A3, ATT["a3"], B3, "a3_prep")

        return counted


def layout(x):
    f = np.float32
    bf = mybir.dt.np(BF16)
    c = np.ascontiguousarray
    w = {}
    swap = np.arange(P) ^ 1

    def pad_o(m):
        o = np.zeros((4, 4, 32, m.shape[1]), f)
        o[:, :, :8] = m.reshape(4, 4, 8, m.shape[1])
        return c(o.reshape(4, P, m.shape[1]).transpose(1, 0, 2))

    def half_swap(n, width):
        i = np.arange(n)
        return (i // width) * width + (i % width + width // 2) % width

    w["x_tm"] = c(x["L0_attn_x"].reshape(TILES, P, D).transpose(1, 0, 2))
    w["one_rows"] = np.ones((2, 2, SEQ), bf)
    w["ident"] = np.eye(P, dtype=f)
    wqkv = x["L0_attn_w_qkv"]
    wq, wk, wv = wqkv[:, :D], wqkv[:, D:2 * D], wqkv[:, 2 * D:]
    w["a0_qk"] = c(np.stack([wq, wq[:, swap], wk, wk[:, swap]], 1))
    w["a0_wv"], w["a0_wo"] = c(wv), pad_o(x["L0_attn_w_o"])
    pos = np.arange(SEQ, dtype=f)
    inv = (f(1) / f(10000) ** (np.arange(4, dtype=f) / f(4))).astype(f)
    ang = (pos[None, :] * inv[(np.arange(P) % 8) // 2][:, None]).astype(f)
    sign = np.where(np.arange(P) % 2 == 0, -1, 1).astype(f)
    w["a0_cos"], w["a0_sin"] = np.cos(ang), np.sin(ang) * sign[:, None]
    w["identb"] = np.eye(P).astype(bf)
    i, j = np.arange(P)[:, None], np.arange(P)[None, :]
    ok = [(i >= j) & (i - j <= 64), i + P - j <= 64, i >= j]
    ok += [o.T for o in ok]
    w["masks"] = c(np.stack([np.where(o, 0.0, -1e30) for o in ok], 1).astype(bf))
    sel = np.zeros((P, 2, P), f)
    for h in range(2):
        sel[h, h] = sel[32 + h, h] = 1
    w["selp"] = sel.astype(bf)
    w["blk64"] = np.kron(np.eye(2), np.ones((64, 64))).astype(f)
    b8 = np.zeros((32, 32), f)
    b8[:8] = 0.125
    w["blk32"] = np.kron(np.eye(4), b8).astype(f)
    den = np.zeros((32, 32), f)
    den[8] = 1
    w["denrow"] = np.kron(np.eye(4), den).astype(f)
    part = half_swap(512, 64)
    for l in range(DEPTH):
        m = x["L0_ffn_wqkv"][l]
        q, k, v = m[:, :512], m[:, 512:1024], m[:, 1024:]
        w[f"f0_qk{l}"] = c(np.stack([q, q[:, part], k, k[:, part]], 1))
        w[f"f0_wv{l}"] = c(v)
        w[f"f0_wo{l}"] = c(x["L0_ffn_wo"][l].reshape(4, P, D).transpose(1, 0, 2))
        w[f"f0_w1{l}"] = c(x["L0_ffn_w1"][l])
        w2 = np.zeros((HCH * P, D), f)
        w2[:HID] = x["L0_ffn_w2"][l]
        w[f"f0_w2{l}"] = c(w2.reshape(HCH, P, D).transpose(1, 0, 2))
        qs, ks = np.tile(x["L0_ffn_q_scale"][l], 2), np.tile(x["L0_ffn_k_scale"][l], 2)
        w[f"f0_vec{l}"] = c(np.stack([qs, qs[part[:P]], ks, ks[part[:P]], x["L0_ffn_ln_g"][l], x["L0_ffn_ln_b"][l],
                                      x["L0_ffn_b2"][l]], 1))
        b1 = np.zeros((2, HCH * P), f)
        b1[0, :HID], b1[1, :HID] = x["L0_ffn_b1"][l][:HID], x["L0_ffn_b1"][l][HID:]
        w[f"f0_b1{l}"] = c(b1.reshape(2 * HCH, P).T)
    hi = np.arange(0, 64, 2, dtype=f)
    invf = (f(1) / f(10000) ** (hi / f(64))).astype(f)
    t = np.arange(SEQ, dtype=f)
    fr = np.tile(invf[:, None] * t[None, :], (4, 1)).astype(f)
    base = ((hi + f(0.4 * 64)) / f(1.4 * 64)).astype(f)
    sc = np.tile((base[:, None] ** ((t - SEQ // 2) / f(32))[None, :]).astype(f), (4, 1))
    sg = np.where(np.arange(P) % 64 < 32, -1, 1).astype(f)[:, None]
    co, si = np.cos(fr), np.sin(fr) * sg
    w["f0_tab"] = c(np.stack([co * sc, si * sc, co / sc, si / sc], 1).astype(f))
    r = half_swap(P, P)
    wq, wk = x["L1_attn_wqr"], x["L1_attn_wkr"]
    bq, bk = x["L1_attn_bqr"], x["L1_attn_bkr"]
    w["a1_qk"] = c(np.stack([wq, wq[:, r], wk, wk[:, r]], 1))
    w["a1_b"] = c(np.stack([bq, bq[r], bk, bk[r], x["L1_attn_bo"]], 1))
    w["a1_wkv"], w["a1_bkv"] = x["L1_attn_wkv"], x["L1_attn_bkv"][:, None]
    w["a1_wv"] = np.concatenate([x["L1_attn_wv"], x["L1_attn_bv"][None, :]], 0)
    w["a1_wo"] = pad_o(x["L1_attn_wo"])
    inv = (f(1) / f(10000) ** (np.arange(0, P, 2, dtype=f) / f(P))).astype(f)
    ang = (pos[None, :] * np.tile(inv, 2)[:, None]).astype(f)
    w["a1_cos"] = np.cos(ang)
    w["a1_sin"] = np.sin(ang) * np.where(np.arange(P) < 64, -1, 1).astype(f)[:, None]
    w["f1_wq"] = x["L1_ffn_w_q"]
    w["f1_gb"] = c(np.stack([x["L1_ffn_bn_gamma"].reshape(16, P).T, x["L1_ffn_bn_beta"].reshape(16, P).T], 1))
    w["f1_keys"] = c(x["L1_ffn_keys"].transpose(3, 2, 0, 1).reshape(P, 16, NK))
    w["f1_down"] = c(x["L1_ffn_down_embed"].T)
    w["f1_up"] = c(x["L1_ffn_up_embed"].reshape(EXPCH, P, D).transpose(1, 0, 2))
    w["iota"] = np.tile(np.arange(NK, dtype=f), (P, 1))
    w["iota_ka"] = np.tile(np.repeat(np.arange(NK), TOPK), (P, 1)).astype(bf)
    w["rankw"] = np.tile(TOPK - np.arange(TOPK), (P, PH)).astype(bf)
    w["f2_w"] = c(x["L2_ffn_weight"].T)
    m = x["L3_attn_w_qkv"]
    w["a3_qk"] = c(np.stack([m[:D].T, m[D:2 * D].T], 1))
    w["a3_wv"], w["a3_wo"] = c(m[2 * D:].T), pad_o(c(x["L3_attn_w_proj"].T))
    sw = np.zeros((4, 32), f)
    sw[:, :8] = x["L3_attn_sub_norm_w"]
    w["a3_vec"] = c(np.stack([sw.reshape(P), x["L3_attn_b_proj"]], 1))
    w["a3_lam"] = c(np.stack([x["L3_attn_lambda_" + n] for n in ("q1", "q2", "k1", "k2")], 1))
    w["f3_wr"] = c(x["L3_ffn_Wr"].T)
    w["f3_w1"] = c(x["L3_ffn_W1"].transpose(2, 0, 1))
    w["f3_b1"] = c(x["L3_ffn_b1"].reshape(32, P).T)
    w["f3_w2"] = c(x["L3_ffn_W2"].reshape(E3, D, 4, P).transpose(3, 0, 2, 1).reshape(P, E3, M3))
    w["f3_b2"] = x["L3_ffn_b2"]
    selw = np.zeros((E3, E3, P), f)
    for e in range(E3):
        selw[e, e] = 1
    w["f3_selw"] = selw
    return {k: c(v if v.dtype == bf else v.astype(f, copy=False)) for k, v in w.items()}


def kernel(**inputs):
    import concourse.bacc as bacc
    from concourse.bass_utils import run_bass_kernel_spmd

    nc = bacc.Bacc("TRN2", target_bir_lowering=False, num_devices=1)
    arrays = layout({k: np.asarray(v) for k, v in inputs.items()})
    w = {k: nc.dram_tensor("in_" + k, a.shape, mybir.dt.from_np(a.dtype), kind="ExternalInput").ap()
         for k, a in arrays.items()}
    out = nc.dram_tensor("result", (BATCH, SEQ, D), F32, kind="ExternalOutput").ap()
    build(nc, w, out)
    r = run_bass_kernel_spmd(nc, [{"in_" + k: a for k, a in arrays.items()}], core_ids=[0])
    return r.results[0]["result"]
```
